# Optimizing a Trainium2 kernel written in Bass

```python
import numpy as np
import jax
import jax.numpy as jnp

def _softmax(x, axis=-1):
    return jax.nn.softmax(x, axis=axis)

def _gelu(x):
    return jax.nn.gelu(x, approximate=True)

def _silu(x):
    return jax.nn.silu(x)

def _sigmoid(x):
    return jax.nn.sigmoid(x)

def _layernorm(x, axis=-1, eps=1e-05):
    m = jnp.mean(x, axis=axis, keepdims=True)
    v = jnp.var(x, axis=axis, keepdims=True)
    return (x - m) / jnp.sqrt(v + eps)

def _scatter_add(tgt, idx, src, axis=0):
    return tgt.at[idx].add(src)

def _segment_sum(src, seg, n):
    return jax.ops.segment_sum(src, seg, n)
kernel_name = 'mk_adj_ffn_d1_adj_r2_8df035'

def setup_inputs(seed: int=0):
    np.random.seed(seed)
    _w = jnp.asarray

    def _rec_inputs():
        import jax
        import jax.numpy as jnp
        _gk = jax.random.key(seed)
        x = 4.136e-05 + 0.9999 * jax.random.normal(jax.random.fold_in(_gk, 1), (4096, 256), jnp.float32)
        _a = jax.random.bernoulli(jax.random.fold_in(_gk, 2), 0.000488281, (4096, 4096))
        _a = jnp.logical_or(_a, jnp.swapaxes(_a, -1, -2))
        _a = jnp.logical_or(_a, jnp.eye(4096, dtype=bool))
        _af = _a.astype(jnp.float32)
        adj = _af
        return (x, adj)
    x, adj = _rec_inputs()

    def _L0_gnn_setup():
        import jax, jax.numpy as jnp
        import numpy as np
        N = 8192
        D_IN = 256
        D_OUT = 256
        AVG_DEG = 32.0
        key = jax.random.key(seed)
        k1, k2, k3, k4 = jax.random.split(key, 4)
        p = AVG_DEG / N
        adjacency = (jax.random.uniform(k1, (N, N)) < p).astype(jnp.float32)
        adjacency = jnp.maximum(adjacency, adjacency.T)
        node_degree = jnp.sum(adjacency, axis=1, keepdims=True) + 1.0
        x = jax.random.normal(k2, (N, D_IN), dtype=jnp.float32)
        W = jax.random.normal(k3, (D_IN, D_OUT), dtype=jnp.float32) * (1.0 / np.sqrt(D_IN))
        b = jax.random.normal(k4, (D_OUT,), dtype=jnp.float32) * 0.01
        return {'x': x, 'adjacency': adjacency, 'node_degree': node_degree, 'W': W, 'b': b}
    _L0_gnn_all = _L0_gnn_setup()
    _L0_gnn_in = {k: v for k, v in _L0_gnn_all.items() if k in ('W', 'b')}
    del _L0_gnn_all

    def _L0_ffn_setup():
        import jax, jax.numpy as jnp
        import numpy as np
        IN_DIM = 256
        HID = 512
        E = 16
        TOPK = 2
        key = jax.random.key(seed)
        ks = jax.random.split(key, 8)
        s = 0.02
        x = jax.random.normal(ks[0], (4, 1024, IN_DIM), dtype=jnp.float32)
        Wr = jax.random.normal(ks[1], (IN_DIM, E), dtype=jnp.float32) * s
        br = jnp.zeros((E,), dtype=jnp.float32)
        W1 = jax.random.normal(ks[2], (E, IN_DIM, HID), dtype=jnp.float32) * s
        b1 = jnp.zeros((E, HID), dtype=jnp.float32)
        W2 = jax.random.normal(ks[3], (E, HID, IN_DIM), dtype=jnp.float32) * s
        b2 = jnp.zeros((E, IN_DIM), dtype=jnp.float32)
        return {'x': x, 'Wr': Wr, 'br': br, 'W1': W1, 'b1': b1, 'W2': W2, 'b2': b2}
    _L0_ffn_all = _L0_ffn_setup()
    _L0_ffn_in = {k: v for k, v in _L0_ffn_all.items() if k in ('Wr', 'br', 'W1', 'b1', 'W2', 'b2')}
    del _L0_ffn_all
    return {'x': x, 'adj': adj, 'L0_gnn_W': _L0_gnn_in['W'], 'L0_gnn_b': _L0_gnn_in['b'], 'L0_ffn_Wr': _L0_ffn_in['Wr'], 'L0_ffn_br': _L0_ffn_in['br'], 'L0_ffn_W1': _L0_ffn_in['W1'], 'L0_ffn_b1': _L0_ffn_in['b1'], 'L0_ffn_W2': _L0_ffn_in['W2'], 'L0_ffn_b2': _L0_ffn_in['b2']}

def reference(x, adj, L0_gnn_W, L0_gnn_b, L0_ffn_Wr, L0_ffn_br, L0_ffn_W1, L0_ffn_b1, L0_ffn_W2, L0_ffn_b2):
    import jax
    import jax.numpy as jnp

    def _L0_gnn_ref(x, adjacency, node_degree, W, b):
        import jax, jax.numpy as jnp
        import numpy as np
        N = 8192
        D_IN = 256
        D_OUT = 256
        AVG_DEG = 32.0
        n = adjacency.shape[0]
        a_hat = adjacency + jnp.eye(n, dtype=adjacency.dtype)
        dinv = jax.lax.rsqrt(node_degree)
        a_norm = dinv * a_hat * dinv
        pooled = a_norm @ x + x
        return jax.nn.relu(pooled @ W + b)

    def _L0_ffn_ref(x, Wr, br, W1, b1, W2, b2):
        import jax, jax.numpy as jnp
        import numpy as np
        IN_DIM = 256
        HID = 512
        E = 16
        TOPK = 2
        token_shape = x.shape[:-1]
        xf = x.reshape(-1, x.shape[-1])
        T = xf.shape[0]
        logits = xf @ Wr + br
        probs = jax.nn.softmax(logits, axis=-1)
        topk_w, topk_idx = jax.lax.top_k(probs, TOPK)
        topk_w = topk_w / jnp.maximum(topk_w.sum(-1, keepdims=True), 1e-09)
        combine = jnp.zeros((T, E), dtype=xf.dtype).at[jnp.arange(T)[:, None], topk_idx].add(topk_w)
        y = jnp.zeros_like(xf)
        for e in range(E):
            h = jax.nn.gelu(xf @ W1[e] + b1[e], approximate=False)
            o = h @ W2[e] + b2[e]
            y = y + combine[:, e:e + 1] * o
        y = xf + y
        return y.reshape(*token_shape, IN_DIM)
    deg = jnp.maximum((adj != 0).astype(jnp.float32).sum(-1), 1.0)
    x = x + _L0_gnn_ref(_layernorm(x, axis=-1), adj, deg[..., None], L0_gnn_W, L0_gnn_b)
    x = x + _L0_ffn_ref(_layernorm(x, axis=-1)[None], L0_ffn_Wr, L0_ffn_br, L0_ffn_W1, L0_ffn_b1, L0_ffn_W2, L0_ffn_b2)[0]
    return x

_drawn_inputs = setup_inputs


def setup_inputs(seed=0):
    import zlib

    import numpy as np

    out = dict(_drawn_inputs(seed))
    spreads = {'L0_ffn_br': (0.0, 0.287), 'L0_ffn_b1': (0.0, 0.8), 'L0_ffn_b2': (0.0, 0.272)}
    factors = {'L0_gnn_b': 8.0}
    for name, (base, spread) in spreads.items():
        noise = np.random.default_rng([zlib.crc32(name.encode()), seed]).standard_normal(out[name].shape)
        drawn = base * np.exp(spread * noise) if base else spread * noise
        out[name] = jnp.asarray(drawn.astype(out[name].dtype))
    for name, factor in factors.items():
        out[name] = (out[name] * factor).astype(out[name].dtype)
    return out
```

```python
from contextlib import ExitStack

import numpy as np

import concourse.bass as bass
from concourse import mybir

ALU = mybir.AluOpType
ACT = mybir.ActivationFunctionType
AX_X = mybir.AxisListType.X
F32 = mybir.dt.float32
F16 = mybir.dt.float16
I32 = mybir.dt.int32
U32 = mybir.dt.uint32

P = 128
N = 4096
D = 256
E = 16
H = 512
TOPK = 2
T = N // P
DC = D // P
HC = H // P
JG = 4
G = T // JG
CH = 4
CW = N // CH
RING = 4
XC = 4
XT = T // XC
HW = D + 2
EPS = 1e-5

CAP = N
BLOCKS = N * TOPK // P + E - 1
QUADS = (BLOCKS + 3) // 4
SPARE = QUADS * 4 - N * TOPK // P
PLACES = E * CAP + SPARE * P
LW = 16

SX = 2.0 ** 11
SW = 2.0 ** 8
SH = 2.0 ** 6

BIG = 1.0e9


def build(nc, x, adj, gnn_W, gnn_b, Wr, br, W1, b1, W2, b2, out):
    ctx = ExitStack()

    def sb(name, shape, dt):
        return ctx.enter_context(nc.sbuf_tensor(name, shape, dt))

    def sem(name):
        return ctx.enter_context(nc.semaphore(name))

    feats = nc.dram_tensor("feats", (N + P, 2 * D), F16, kind="Internal").ap()
    lists = nc.dram_tensor("lists", (PLACES, LW), I32, kind="Internal").ap()
    total = nc.dram_tensor("total", (N + P, D), F32, kind="Internal").ap()

    w1h = sb("w1h", [P, E * DC * H], F16)
    w1l = sb("w1l", [P, E * DC * H], F16)
    w2h = sb("w2h", [P, E * HC * D], F16)
    w2l = sb("w2l", [P, E * HC * D], F16)
    xin = w2h[:, :].bitcast(F32).rearrange("p (n d) -> p n d", d=D)
    xin2 = w2l[:, :].bitcast(F32).rearrange("p (n d) -> p n d", d=D)
    pads = w1l[:, :].bitcast(I32).rearrange("p (q w) -> p q w", w=LW)
    pads2 = w1h[:, 0:SPARE * LW * 2].bitcast(I32).rearrange("p (q w) -> p q w", w=LW)
    xparts = sb("xparts", [P, T * (HW + D)], F16)
    xh = xparts[:, 0:T * HW].rearrange("p (n w) -> p n w", w=HW)
    xl = xparts[:, T * HW:T * (HW + D)].rearrange("p (n w) -> p n w", w=D)
    b1all = xparts[:, 0:2 * E * H].bitcast(F32)
    abuf = sb("abuf", [P, CH * CW], F32)
    xg = [abuf[:, k * D:(k + 1) * D].bitcast(F16) for k in range(4)]
    hb = [abuf[:, 1024 + k * H:1024 + (k + 1) * H] for k in range(2)]
    hg = [abuf[:, 2048 + k * H:2048 + (k + 1) * H] for k in range(2)]
    orow = [abuf[:, 3072 + k * D:3072 + (k + 1) * D] for k in range(4)]
    at = sb("at", [P, RING, JG * P], F16)
    wst = sb("wst", [P, DC * H], F32)
    xgT, hh = at[:, 0:2, :], at[:, 2:4, :]
    hl = sb("hl", [P, 2, H], F16)
    info = sb("info", [P, 4, 2], I32)

    wg = sb("wg", [P, DC, D], F32)
    gb = sb("gb", [P, D], F32)
    wr = sb("wr", [P, DC, E], F32)
    brb = sb("brb", [P, E], F32)
    b2s = sb("b2s", [E, D], F32)
    id32 = sb("id32", [P, P], F32)
    id16 = sb("id16", [P, P], F16)
    before = sb("before", [P, P], F16)
    ones16 = sb("ones16", [P, P], F16)
    iota_e = sb("iota_e", [P, E], F32)
    iota_p = sb("iota_p", [P, 1], F32)
    thr = sb("thr", [P, T], F32)
    mhalf = sb("mhalf", [P, XT], F32)
    zrow = sb("zrow", [P, D], F32)

    mean = sb("mean", [P, T], F32)
    rstd = sb("rstd", [P, T], F32)
    st6 = sb("st6", [P, XC, XT, 6], F32)
    var8 = sb("var8", [P, XC, XT], F32)
    dif8 = sb("dif8", [P, XT], F32)

    xt = sb("xt", [P, 2, D], F32)
    xs = sb("xs", [P, D], F32)
    pooled = sb("pooled", [P, D], F32)
    eT = sb("eT", [P, D], F32)
    x1 = sb("x1", [P, D], F32)
    xf = sb("xf", [P, D], F32)
    pay = sb("pay", [P, 2 * D], F16)
    base = sb("base", [P, 2, D], F32)
    dinv2 = sb("dinv2", [P, 2], F32)
    bst = sb("bst", [P, 6], F32)
    mv = sb("mv", [P, 2], F32)
    vr = sb("vr", [P, 2], F32)
    lg = sb("lg", [P, E], F32)
    ex = sb("ex", [P, E], F32)
    pr = sb("pr", [P, E], F32)
    m8 = sb("m8", [P, 8], F32)
    p8 = sb("p8", [P, 8], F32)
    i8 = sb("i8", [P, 8], U32)
    sc = sb("sc", [P, 8], F32)
    i2 = sb("i2", [P, 2], F32)
    oh = sb("oh", [P, 2, E], F32)
    msk = sb("msk", [P, E], F16)
    cmb = sb("cmb", [P, E], F32)
    cT = sb("cT", [E, P], F32)
    run = sb("run", [P, E], F32)
    posb = sb("posb", [P, E], F32)
    junk = sb("junk", [P, 2, E], F32)
    posf = sb("posf", [P, 2], F32)
    posi = sb("posi", [P, 2], I32)
    tok = sb("tok", [P, 1], F32)
    place = sb("place", [P, 2, LW], I32)

    cnt = sb("cnt", [P, E], F32)
    nblk = sb("nblk", [P, E], F32)
    cum = sb("cum", [P, E], F32)
    tri = sb("tri", [P, E, E], F32)
    tbl = sb("tbl", [P, 8], F32)
    tabi = sb("tabi", [P, 2], I32)
    tab = wst[0:1, E * T + E * E:E * T + E * E + 2 * P].bitcast(I32)
    over = wst[:, 0:E * T].rearrange("p (e m) -> p e m", m=T)
    tmp3 = wst[:, E * T:E * T + E * E].rearrange("p (e f) -> p e f", f=E)

    banks = [ctx.enter_context(nc.psum_tensor(f"bank{i}", [P, 512], F32)) for i in range(8)]
    ps_tp = banks[0:2]
    ps_acc = banks[2:4]
    ps_T, ps_Z, ps_S, ps_B = banks[4:8]
    q_x = [b[:, :].bitcast(F16) for b in banks[0:2]]
    q_h = banks[2:4]
    q_g = banks[4:6]
    q_o = banks[6:8]

    S = {}

    def ev(name):
        if name not in S:
            S[name] = sem(name)
        return S[name]

    def after(eng, name, t):
        eng.wait_ge(ev(name), t + 1)

    def passed(eng, name):
        eng.sem_inc(ev(name + "_passed"), 1)

    x_in = [sem(f"x_in{c}") for c in range(XC)]
    a_in = [sem(f"a_in{c}") for c in range(CH)]
    xt_in = [sem(f"xt_in{c}") for c in range(2)]
    lst_in = [sem(f"lst_in{c}") for c in range(4)]
    xg_in = [sem(f"xg_in{c}") for c in range(4)]
    added = [sem(f"added{c}") for c in range(4)]

    def landed(eng, sems, q, r):
        eng.wait_ge(sems[r], (q + 1) * 16)

    x_v = x.rearrange("(n p) d -> p n d", p=P)
    consts = [(wg[:, :, :], gnn_W.rearrange("(c p) n -> p c n", p=P)),
              (wr[:, :, :], Wr.rearrange("(c p) n -> p c n", p=P)),
              (b2s[:, :], b2),
              (gb[:, :], gnn_b.rearrange("(a d) -> a d", a=1).broadcast_to([P, D])),
              (brb[:, :], br.rearrange("(a d) -> a d", a=1).broadcast_to([P, E]))]

    def step_up(t, g, k):
        return t + (g + k) // G, (g + k) % G

    def over_tiles(eng, step):
        for t in (0, 1):
            step(t, t)
        with eng.Fori(1, T // 2 - 1) as i:
            step(i * 2, 0)
            step(i * 2 + 1, 1)
        for t in range(T - 2, T + 2):
            step(t, t % 2)

    def is_(t, cond):
        return cond(t) if isinstance(t, int) else True

    def over_blocks(eng, step):
        for r in range(4):
            step(0, r)
        with eng.Fori(1, QUADS - 1) as q:
            for r in range(4):
                step(q, r)
        for r in range(BLOCKS + 2 - 4 * (QUADS - 1)):
            step(QUADS - 1, r)

    def shift(q, r, k):
        return q + (r + k) // 4, (r + k) % 4

    def exists(q, r):
        return not isinstance(q, int) or 0 <= 4 * q + r < BLOCKS

    def blk(q, r):
        return q * 4 + r

    block = ctx.enter_context(nc.Block())

    @block.sync
    def _(sp):
        for dst, src in consts[0:2]:
            sp.dma_start(dst, src).then_inc(ev("consts_in"), 16)
        for c in range(XC):
            sp.dma_start(xin[:, c * XT:(c + 1) * XT, :] if c < 2 else xin2[:, (c - 2) * XT:(c - 1) * XT, :],
                         x_v[:, c * XT:(c + 1) * XT, :]).then_inc(x_in[c], 16)
            sp.dma_start(abuf[:, c * CW:(c + 1) * CW], adj[0:P, c * CW:(c + 1) * CW]).then_inc(a_in[c], 16)
        for dst, src in consts[2:]:
            sp.dma_start(dst, src).then_inc(ev("consts_in"), 16)

        def load_adj(t, c):
            sp.wait_ge(ev("transposed"), t * G - G + 2 * c + 2)
            sp.dma_start(abuf[:, c * CW:(c + 1) * CW],
                         adj[bass.ds(t * P, P), c * CW:(c + 1) * CW]).then_inc(a_in[c], 16)

        def load_weights(t, odd):
            if is_(t, lambda t: t > 0):
                after(sp, "w_cut", t - 1)
            if odd:
                e = t // 2
                sp.dma_start(wst[:, :].rearrange("p (c n) -> p c n", c=HC),
                             W2[bass.ds(e, 1), :, :].rearrange("a (c p) n -> p (a c) n", p=P)).then_inc(ev("w_in"), 16)
            else:
                e = t // 2
                sp.dma_start(wst[:, :].rearrange("p (c n) -> p c n", c=DC),
                             W1[bass.ds(e, 1), :, :].rearrange("a (c p) n -> p (a c) n", p=P)).then_inc(ev("w_in"), 16)

        def step(t, odd):
            if is_(t, lambda t: t >= T):
                return
            if is_(t, lambda t: t > 0):
                for c in range(CH):
                    load_adj(t, c)
            if is_(t, lambda t: t >= 2):
                after(sp, "x1_made", t - 2)
            sp.dma_start(xt[:, odd, :], x[bass.ds(t * P, P), :]).then_inc(xt_in[odd], 16)
            load_weights(t, odd)

        def step_i(t, odd):
            step(t, odd)

        for t in (0, 1):
            step_i(t, t)
        with sp.Fori(1, T // 2) as i:
            for odd in (0, 1):
                t = i * 2 + odd
                for c in range(CH):
                    load_adj(t, c)
                after(sp, "x1_made", t - 2)
                sp.dma_start(xt[:, odd, :], x[bass.ds(t * P, P), :]).then_inc(xt_in[odd], 16)
                after(sp, "w_cut", t - 1)
                W, c = ((W1, DC), (W2, HC))[odd]
                sp.dma_start(wst[:, :].rearrange("p (c n) -> p c n", c=c),
                             W[bass.ds(i, 1), :, :].rearrange("a (c p) n -> p (a c) n", p=P)).then_inc(ev("w_in"), 16)

        sp.wait_ge(ev("multiplied"), T * G)
        sp.dma_start(b1all, b1.rearrange("(a e) h -> a (e h)", a=1).broadcast_to([P, E * H])).then_inc(ev("b1_in"), 16)
        sp.wait_ge(ev("table_made"), 1)
        sp.dma_start(tab[0:1, :], tabi[:, :]).then_inc(ev("table_in"), 16)
        sp.wait_ge(ev("table_in"), 16)
        sp.wait_ge(ev("listed"), 16 * 2 * T)

        def load_list(q, r):
            if not isinstance(q, int) or q > 0:
                landed(sp, added, q - 1, r)
            row = sp.value_load(tab[0:1, bass.ds(blk(q, r) * 2, 1)], min_val=0, max_val=PLACES - P)
            sp.dma_start(info[:, r, :], lists[bass.ds(row, P), 0:2]).then_inc(lst_in[r], 16)

        for r in range(4):
            load_list(0, r)
        with sp.Fori(1, QUADS - 1) as q:
            for r in range(4):
                load_list(q, r)
        for r in range(BLOCKS - 4 * (QUADS - 1)):
            load_list(QUADS - 1, r)

        q, r = divmod(BLOCKS - 1, 4)
        landed(sp, added, q, r)
        sp.dma_start(out[0:N // 2, :], total[0:N // 2, :]).then_inc(ev("out_done"), 16)
        sp.dma_start(out[N // 2:N, :], total[N // 2:N, :]).then_inc(ev("out_done"), 16)
        sp.wait_ge(ev("out_done"), 32)

    @block.tensor
    def _(pe):
        def transposes(t, g):
            if g % 2 == 0:
                landed(pe, a_in, t, g // 2)
            for j in range(JG):
                k = g * JG + j
                mm = pe.transpose(ps_tp[g % 2][:, j * P:(j + 1) * P], abuf[:, k * P:(k + 1) * P], id32[:, :])
            mm.then_inc(ev("transposed"), 1)

        def pooled_T(s):
            after(pe, "pooled", s)
            for c in range(DC):
                mm = pe.transpose(ps_T[:, c * P:(c + 1) * P], pooled[:, c * P:(c + 1) * P], id32[:, :])
            mm.then_inc(ev("pooled_T"), 1)

        def graph_out(s):
            after(pe, "pooled_T_copied", s)
            for c in range(DC):
                mm = pe.matmul(ps_Z[:, 0:D], eT[:, c * P:(c + 1) * P], wg[:, c, :], start=c == 0, stop=c == DC - 1)
            mm.then_inc(ev("graph_out"), 1)

        def xf_T(s):
            after(pe, "xf_made", s)
            for c in range(DC):
                mm = pe.transpose(ps_T[:, D + c * P:D + (c + 1) * P], xf[:, c * P:(c + 1) * P], id32[:, :])
            mm.then_inc(ev("xf_T"), 1)

        def logits(s):
            after(pe, "xf_T_copied", s)
            if is_(s, lambda s: s >= 1):
                after(pe, "run_counted", s - 1)
            for c in range(DC):
                mm = pe.matmul(ps_S[:, 0:E], eT[:, c * P:(c + 1) * P], wr[:, c, :], start=c == 0, stop=c == DC - 1)
            mm.then_inc(ev("logits"), 1)

        def rank(s):
            after(pe, "combine_made", s)
            pe.matmul(ps_S[:, E:2 * E], before[:, :], msk[:, :], start=True, stop=True)
            pe.matmul(ps_S[:, 2 * E:3 * E], ones16[:, :], msk[:, :], start=True, stop=True)
            if is_(s, lambda s: s >= 1):
                after(pe, "base_made", s - 1)
            pe.transpose(ps_B[0:E, D:D + P], cmb[:, :], id32[:, :]).then_inc(ev("ranked"), 1)

        def bias2(s):
            after(pe, "combine_T_copied", s)
            pe.matmul(ps_B[:, 0:D], cT[:, :], b2s[:, :], start=True, stop=True).then_inc(ev("bias2"), 1)

        def step(t, odd):
            s, r = t - 1, t - 2
            has_t = is_(t, lambda t: t < T)
            has_s = is_(s, lambda s: 0 <= s < T)
            has_r = is_(r, lambda r: 0 <= r < T)
            for g in range(G):
                if has_t:
                    pe.wait_ge(ev("at_odd" if g % 2 else "at_even"), t * (G // 2) + g // 2 + 1)
                    t2, g2 = step_up(t, g, 2)
                    if is_(t2, lambda t2: t2 < T):
                        transposes(t2, g2)
                    if g == 0 and is_(t, lambda t: t >= 2):
                        after(pe, "acc_read", t - 2)
                    if isinstance(t, int) and t == 0 and g % (XT // JG) == 0:
                        after(pe, "xparts_made", g // (XT // JG))
                    for j in range(g * JG, (g + 1) * JG):
                        w = at[:, g % RING, (j % JG) * P:(j % JG + 1) * P]
                        last = j == T - 1
                        pe.matmul(ps_acc[odd][:, 0:D], w, xl[:, j, :], start=False, stop=False,
                                  skip_group_check=True) if j else None
                        mm = pe.matmul(ps_acc[odd][:, 0:D + 1], w, xh[:, j, 0:D + 1], start=j == 0, stop=last)
                        if j == 0:
                            mm = pe.matmul(ps_acc[odd][:, 0:D], w, xl[:, j, :], start=False, stop=False)
                    mm.then_inc(ev("multiplied"), 1)
                if g == 0 and has_r:
                    logits(r)
                if g == 1 and has_s:
                    pooled_T(s)
                if g == 3 and has_s:
                    graph_out(s)
                if g == 4 and has_r:
                    rank(r)
                if g == 6 and has_r:
                    bias2(r)
                if g == 7 and has_s:
                    xf_T(s)

        pe.wait_ge(ev("ids_made"), 1)
        transposes(0, 0)
        transposes(0, 1)
        pe.wait_ge(ev("consts_in"), 16 * len(consts))
        over_tiles(pe, step)

        def tokens_T(q, r):
            landed(pe, xg_in, q, r)
            if not isinstance(q, int) or blk(q, r) >= 2:
                after(pe, "tokens_T_copied", blk(q, r) - 2)
            for c in range(2 * DC):
                mm = pe.transpose(q_x[r % 2][:, c * P:(c + 1) * P], xg[r][:, c * P:(c + 1) * P], id16[:, :])
            mm.then_inc(ev("tokens_T"), 1)

        def hidden(q, r):
            after(pe, "tokens_T_copied", blk(q, r))
            if not isinstance(q, int) or blk(q, r) >= 2:
                after(pe, "biased", blk(q, r) - 2)
            passed(pe, "block")
            e = pe.value_load(tab[0:1, bass.ds(blk(q, r) * 2 + 1, 1)], min_val=0, max_val=E - 1)
            n = 0
            for c in range(DC):
                high = xgT[:, r % 2, c * P:(c + 1) * P]
                low = xgT[:, r % 2, D + c * P:D + (c + 1) * P]
                wh = w1h[:, bass.ds(e * (DC * H) + c * H, H)]
                wl = w1l[:, bass.ds(e * (DC * H) + c * H, H)]
                for a, w in ((high, wh), (high, wl), (low, wh)):
                    mm = pe.matmul(q_h[r % 2][:, :], a, w, start=n == 0, stop=n == 3 * DC - 1)
                    n += 1
            mm.then_inc(ev("hidden"), 1)

        def hidden_T(q, r):
            after(pe, "gelued", blk(q, r))
            if not isinstance(q, int) or blk(q, r) >= 2:
                after(pe, "low_cut", blk(q, r) - 2)
            for c in range(HC):
                mm = pe.transpose(q_g[r % 2][:, c * P:(c + 1) * P], hg[r % 2][:, c * P:(c + 1) * P], id32[:, :])
            mm.then_inc(ev("hidden_T"), 1)

        def expert_out(q, r):
            after(pe, "low_cut", blk(q, r))
            if not isinstance(q, int) or blk(q, r) >= 2:
                after(pe, "weighted", blk(q, r) - 2)
            passed(pe, "block")
            e = pe.value_load(tab[0:1, bass.ds(blk(q, r) * 2 + 1, 1)], min_val=0, max_val=E - 1)
            n = 0
            for c in range(HC):
                high, low = hh[:, r % 2, c * P:(c + 1) * P], hl[:, r % 2, c * P:(c + 1) * P]
                wh = w2h[:, bass.ds(e * (HC * D) + c * D, D)]
                wl = w2l[:, bass.ds(e * (HC * D) + c * D, D)]
                for a, w in ((high, wh), (high, wl), (low, wh)):
                    mm = pe.matmul(q_o[r % 2][:, 0:D], a, w, start=n == 0, stop=n == 3 * HC - 1)
                    n += 1
            mm.then_inc(ev("expert_out"), 1)

        pe.wait_ge(ev("table_in"), 16)
        after(pe, "base_made", T - 1)
        after(pe, "run_counted", T - 1)
        tokens_T(0, 0)

        def bstep(q, r):
            prev, nxt = shift(q, r, -1), shift(q, r, 1)
            if exists(*prev):
                hidden_T(*prev)
            if exists(q, r):
                hidden(q, r)
            if exists(*nxt):
                tokens_T(*nxt)
            if exists(*prev):
                expert_out(*prev)

        over_blocks(pe, bstep)

    @block.scalar
    def _(act):
        def copy_group(t, g):
            act.wait_ge(ev("transposed"), t * G + g + 1)
            if is_(t, lambda t: t * G + g >= RING):
                act.wait_ge(ev("multiplied"), t * G + g - RING + 1)
            act.activation(at[:, g % RING, :], ps_tp[0][:, :], ACT.Copy).then_inc(ev("at_even"), 1)

        def copy_pooled_T(s):
            after(act, "pooled_T", s)
            if is_(s, lambda s: s >= 1):
                after(act, "logits", s - 1)
            act.activation(eT[:, :], ps_T[:, 0:D], ACT.Copy).then_inc(ev("pooled_T_copied"), 1)

        def copy_xf_T(s):
            after(act, "xf_T", s)
            act.activation(eT[:, :], ps_T[:, D:2 * D], ACT.Copy).then_inc(ev("xf_T_copied"), 1)

        def high_part(s):
            after(act, "xf_made", s)
            if is_(s, lambda s: s >= 1):
                after(act, "feats_out", s * 16 - 1)
            act.activation(pay[:, 0:D], xf[:, :], ACT.Copy).then_inc(ev("high_made"), 1)

        def exps(s):
            after(act, "max_made", s)
            act.activation(ex[:, :], lg[:, :], ACT.Exp, bias=sc[:, 0:1], accum_out=sc[:, 1:2])\
               .then_inc(ev("exps_made"), 1)

        def copy_combine_T(s):
            after(act, "ranked", s)
            if is_(s, lambda s: s >= 1):
                after(act, "bias2", s - 1)
            act.activation(cT[:, :], ps_B[0:E, D:D + P], ACT.Copy).then_inc(ev("combine_T_copied"), 1)

        for c in range(XC):
            after(act, "x_scaled", c)
            src = (xin if c < 2 else xin2)[:, (c % 2) * XT:(c % 2 + 1) * XT, :]
            act.activation(xh[:, c * XT:(c + 1) * XT, 0:D], src, ACT.Copy).then_inc(ev("xh_made"), 1)
            if c == 0:
                copy_group(0, 0)

        def step(t, odd):
            s, r = t - 1, t - 2
            has_s = is_(s, lambda s: 0 <= s < T)
            has_r = is_(r, lambda r: 0 <= r < T)
            for g in range(G):
                if g == 0 and has_r:
                    copy_xf_T(r)
                if g % 2 == 0:
                    t2, g2 = step_up(t, g, 2)
                    if is_(t2, lambda t2: t2 < T):
                        copy_group(t2, g2)
                if g == 1 and has_r:
                    exps(r)
                if g == 2 and has_s:
                    copy_pooled_T(s)
                if g == 5 and has_r:
                    copy_combine_T(r)
                if g == 7 and has_s:
                    high_part(s)

        over_tiles(act, step)

        def gelu(q, r):
            after(act, "biased", blk(q, r))
            if not isinstance(q, int) or blk(q, r) >= 2:
                after(act, "hidden_T", blk(q, r) - 2)
            act.activation(hg[r % 2], hb[r % 2], ACT.Gelu).then_inc(ev("gelued"), 1)

        def cut_high(q, r):
            after(act, "hidden_T", blk(q, r))
            if not isinstance(q, int) or blk(q, r) >= 2:
                after(act, "expert_out", blk(q, r) - 2)
            act.activation(hh[:, r % 2, :], q_g[r % 2][:, :], ACT.Copy, scale=SH).then_inc(ev("high_cut"), 1)

        def weigh(q, r):
            after(act, "expert_out", blk(q, r))
            if not isinstance(q, int) or q >= 1:
                landed(act, added, q - 1, r)
            act.activation(orow[r], q_o[r % 2][:, 0:D], ACT.Copy,
                           scale=info[:, r, 1:2].bitcast(F32)).then_inc(ev("weighted"), 1)

        def bstep(q, r):
            prev = shift(q, r, -1)
            if exists(*prev):
                cut_high(*prev)
            if exists(q, r):
                gelu(q, r)
            if exists(*prev):
                weigh(*prev)

        over_blocks(act, bstep)

    @block.vector
    def _(dve):
        V = dve

        def tile_of(c):
            return (xin if c < 2 else xin2), (c % 2) * XT

        def stats(c):
            src, k0 = tile_of(c)
            V.wait_ge(x_in[c], 16)
            with V.Fori(0, XT) as k:
                V.bn_stats(st6[:, c, bass.ds(k, 1), :], src[:, bass.ds(k + k0, 1), :]).then_inc(ev("bn"), 1)
            V.wait_ge(ev("bn"), XT * (c + 1))
            m_e, m_o = st6[:, c, :, 1], st6[:, c, :, 4]
            v_e, v_o = st6[:, c, :, 2], st6[:, c, :, 5]
            V.tensor_tensor(mean[:, c * XT:(c + 1) * XT], m_e, m_o, ALU.add).then_inc(ev("mean_sum"), 1)
            V.tensor_tensor(dif8[:, :], m_e, m_o, ALU.subtract).then_inc(ev("dif"), 1)
            V.tensor_tensor(var8[:, c, :], v_e, v_o, ALU.add).then_inc(ev("var_sum"), 1)
            after(V, "mean_sum", c)
            V.tensor_scalar(mean[:, c * XT:(c + 1) * XT], mean[:, c * XT:(c + 1) * XT], 0.5, None, ALU.mult)\
             .then_inc(ev("mean_made"), 1)
            after(V, "dif", c)
            V.tensor_tensor(dif8[:, :], dif8[:, :], dif8[:, :], ALU.mult).then_inc(ev("dif2"), 1)
            after(V, "dif2", c)
            after(V, "var_sum", c)
            V.scalar_tensor_tensor(out=var8[:, c, :], in0=dif8[:, :], scalar=D / 4.0, in1=var8[:, c, :],
                                   op0=ALU.mult, op1=ALU.add).then_inc(ev("var_made"), 1)
            after(V, "var_made", c)
            V.tensor_scalar(var8[:, c, :], var8[:, c, :], 1.0 / D, EPS, ALU.mult, ALU.add)\
             .then_inc(ev("var_eps"), 1)
            after(V, "var_eps", c)
            V.tensor_scalar(var8[:, c, :], var8[:, c, :], SX ** -2, None, ALU.mult).then_inc(ev("var_ready"), 1)

        def scale_x(c):
            src, k0 = tile_of(c)
            after(V, "rstd_made", c)
            after(V, "mean_made", c)
            with V.Fori(0, XT) as k:
                V.tensor_scalar(src[:, bass.ds(k + k0, 1), :], src[:, bass.ds(k + k0, 1), :],
                                mean[:, bass.ds(k + c * XT, 1)], rstd[:, bass.ds(k + c * XT, 1)],
                                ALU.subtract, ALU.mult).then_inc(ev("x_tiles"), 1)
            V.wait_ge(ev("x_tiles"), XT * (c + 1))
            V.engine_nop().then_inc(ev("x_scaled"), 1) if False else \
                V.memset(junk[:, :, :], 0.0).then_inc(ev("x_scaled"), 1)

        V.memset(zrow[:, :], 0.0).then_inc(ev("zeros_made"), 1)
        V.memset(xh[:, :, D:D + 2], 1.0).then_inc(ev("ones_made"), 1)

        def copy_group(t, g):
            V.wait_ge(ev("transposed"), t * G + g + 1)
            if is_(t, lambda t: t * G + g >= RING):
                V.wait_ge(ev("multiplied"), t * G + g - RING + 1)
            V.tensor_copy(at[:, g % RING, :], ps_tp[1][:, :]).then_inc(ev("at_odd"), 1)

        stats(0)
        for c in range(XC):
            if c + 1 < XC:
                stats(c + 1)
            scale_x(c)
        copy_group(0, 1)

        def pool_x(s, odd):
            V.wait_ge(xt_in[odd], s // 2 * 16 + 16 if isinstance(s, int) else (s - odd) * 8 + 16)
            if is_(s, lambda s: s >= 1):
                after(V, "pooled", s - 1)
            V.tensor_scalar(xs[:, :], xt[:, odd, :], mean[:, bass.ds(s, 1)], rstd[:, bass.ds(s, 1)],
                            ALU.subtract, ALU.mult).then_inc(ev("xs_made"), 1)
            V.wait_ge(ev("multiplied"), s * G + G)
            V.tensor_scalar(dinv2[:, 0:1], ps_acc[odd][:, D:D + 1], 1.0, None, ALU.max).then_inc(ev("degree"), 1)
            after(V, "degree", s)
            V.reciprocal(dinv2[:, 1:2], dinv2[:, 0:1]).then_inc(ev("dinv2"), 1)
            after(V, "xs_made", s)
            if is_(s, lambda s: s >= 1):
                after(V, "pooled_T", s - 1)
            V.tensor_tensor(pooled[:, :], ps_acc[odd][:, 0:D], xs[:, :], ALU.add).then_inc(ev("acc_read"), 1)
            after(V, "acc_read", s)
            after(V, "dinv2", s)
            V.scalar_tensor_tensor(out=pooled[:, :], in0=pooled[:, :], scalar=dinv2[:, 1:2], in1=xs[:, :],
                                   op0=ALU.mult, op1=ALU.add).then_inc(ev("pooled"), 1)

        def graph_add(s, odd):
            after(V, "graph_out", s)
            V.scalar_tensor_tensor(out=x1[:, :], in0=ps_Z[:, 0:D], scalar=1.0 / SX, in1=gb[:, :],
                                   op0=ALU.mult, op1=ALU.add).then_inc(ev("graph_biased"), 1)
            after(V, "graph_biased", s)
            V.scalar_tensor_tensor(out=x1[:, :], in0=x1[:, :], scalar=0.0, in1=xt[:, odd, :],
                                   op0=ALU.max, op1=ALU.add).then_inc(ev("x1_made"), 1)
            after(V, "x1_made", s)
            V.bn_stats(bst[:, :], x1[:, :]).then_inc(ev("x1_stats"), 1)
            after(V, "x1_stats", s)
            passed(V, "x1_stats")
            V.bn_aggr(mv[:, :], bst[:, :]).then_inc(ev("x1_aggr"), 1)
            after(V, "x1_aggr", s)
            V.tensor_scalar(vr[:, 0:1], mv[:, 1:2], EPS, SX ** -2, ALU.add, ALU.mult).then_inc(ev("x1_var"), 1)

        def norm_x1(s, odd):
            after(V, "x1_rstd", s)
            if is_(s, lambda s: s >= 1):
                after(V, "low_made", s - 1)
            V.tensor_scalar(xf[:, :], x1[:, :], mv[:, 0:1], vr[:, 1:2], ALU.subtract, ALU.mult)\
             .then_inc(ev("xf_made"), 1)
            after(V, "xf_made", s)
            if is_(s, lambda s: s >= 2):
                after(V, "total_out", (s - 1) * 16 - 1)
            V.scalar_tensor_tensor(out=base[:, odd, :], in0=xf[:, :], scalar=1.0 / SX, in1=x1[:, :],
                                   op0=ALU.mult, op1=ALU.add).then_inc(ev("residual_made"), 1)

        def top1(s):
            after(V, "logits", s)
            V.scalar_tensor_tensor(out=lg[:, :], in0=ps_S[:, 0:E], scalar=1.0 / SX, in1=brb[:, :],
                                   op0=ALU.mult, op1=ALU.add).then_inc(ev("lg_made"), 1)
            after(V, "lg_made", s)
            V.tensor_reduce(m8[:, 0:1], lg[:, :], AX_X, ALU.max).then_inc(ev("max_found"), 1)
            after(V, "max_found", s)
            V.tensor_scalar(sc[:, 0:1], m8[:, 0:1], -1.0, None, ALU.mult).then_inc(ev("max_made"), 1)

        def top2(s):
            after(V, "exps_made", s)
            V.reciprocal(sc[:, 2:3], sc[:, 1:2]).then_inc(ev("sum_inv"), 1)
            after(V, "sum_inv", s)
            V.tensor_scalar(pr[:, :], ex[:, :], sc[:, 2:3], None, ALU.mult).then_inc(ev("probs"), 1)
            after(V, "probs", s)
            passed(V, "probs")
            V.max(p8[:, :], pr[:, :]).then_inc(ev("top_p"), 1)
            after(V, "top_p", s)
            passed(V, "top_p")
            V.max_index(i8[:, :], p8[:, :], pr[:, :]).then_inc(ev("top_i"), 1)
            V.tensor_scalar(sc[:, 3:4], p8[:, 0:1], p8[:, 1:2], 1e-9, ALU.add, ALU.max).then_inc(ev("top_sum"), 1)
            after(V, "top_sum", s)
            V.reciprocal(sc[:, 4:5], sc[:, 3:4]).then_inc(ev("top_inv"), 1)
            after(V, "top_i", s)
            V.tensor_copy(i2[:, :], i8[:, 0:2]).then_inc(ev("top_if"), 1)
            after(V, "top_inv", s)
            V.tensor_scalar(sc[:, 5:7], p8[:, 0:2], sc[:, 4:5], None, ALU.mult).then_inc(ev("top_w"), 1)
            after(V, "top_if", s)
            V.tensor_scalar(oh[:, 0, :], iota_e[:, :], i2[:, 0:1], None, ALU.is_equal).then_inc(ev("hot0"), 1)
            V.tensor_scalar(oh[:, 1, :], iota_e[:, :], i2[:, 1:2], None, ALU.is_equal).then_inc(ev("hot1"), 1)
            after(V, "hot1", s)
            after(V, "hot0", s)
            V.tensor_tensor(msk[:, :], oh[:, 0, :], oh[:, 1, :], ALU.add).then_inc(ev("mask_made"), 1)
            after(V, "top_w", s)
            V.tensor_scalar(cmb[:, :], oh[:, 0, :], sc[:, 5:6], None, ALU.mult).then_inc(ev("combine0"), 1)
            after(V, "combine0", s)
            V.scalar_tensor_tensor(out=cmb[:, :], in0=oh[:, 1, :], scalar=sc[:, 6:7], in1=cmb[:, :],
                                   op0=ALU.mult, op1=ALU.add).then_inc(ev("combine_made"), 1)

        def places(s):
            after(V, "ranked", s)
            V.tensor_tensor(posb[:, :], ps_S[:, E:2 * E], run[:, :], ALU.add).then_inc(ev("place_base"), 1)
            after(V, "place_base", s)
            V.tensor_tensor(run[:, :], ps_S[:, 2 * E:3 * E], run[:, :], ALU.add).then_inc(ev("run_counted"), 1)
            for k in range(TOPK):
                V.tensor_tensor_reduce(out=junk[:, k, :], in0=posb[:, :], in1=oh[:, k, :], scale=1.0, scalar=0.0,
                                       op0=ALU.mult, op1=ALU.add, accum_out=posf[:, k:k + 1])\
                 .then_inc(ev(f"place{k}"), 1)
            if is_(s, lambda s: s >= 1):
                after(V, "listed", s * 32 - 1)
            V.tensor_copy(place[:, :, 0], tok[:, :].broadcast_to([P, TOPK])).then_inc(ev("token_put"), 1)
            V.tensor_scalar(place[:, :, 1].bitcast(F32), sc[:, 5:7], 1.0 / (SH * SW), None, ALU.mult)\
             .then_inc(ev("weight_put"), 1)
            after(V, "token_put", s)
            V.tensor_scalar(tok[:, :], tok[:, :], float(P), None, ALU.add).then_inc(ev("token_next"), 1)
            after(V, "place0", s)
            after(V, "place1", s)
            V.tensor_copy(posi[:, :], posf[:, :]).then_inc(ev("placed"), 1)

        def finish_base(s, odd):
            after(V, "bias2", s)
            after(V, "residual_made", s)
            V.tensor_tensor(base[:, odd, :], ps_B[:, 0:D], base[:, odd, :], ALU.add).then_inc(ev("base_made"), 1)

        V.wait_ge(ev("ids_made"), 1)
        V.wait_ge(ev("consts_in"), 16 * len(consts))

        def step(t, odd):
            s, r = t - 1, t - 2
            has_s = is_(s, lambda s: 0 <= s < T)
            has_r = is_(r, lambda r: 0 <= r < T)
            for g in range(G):
                if g % 2 == 1:
                    t2, g2 = step_up(t, g, 2)
                    if is_(t2, lambda t2: t2 < T):
                        copy_group(t2, g2)
                if g == 0 and has_s:
                    pool_x(s, 1 - odd)
                if g == 1 and has_r:
                    top1(r)
                if g == 2 and has_r:
                    top2(r)
                if g == 4 and has_s:
                    graph_add(s, 1 - odd)
                if g == 5 and has_r:
                    places(r)
                if g == 6 and has_s:
                    norm_x1(s, 1 - odd)
                if g == 7 and has_r:
                    finish_base(r, odd)

        over_tiles(V, step)

        after(V, "run_counted", T - 1)
        V.tensor_tensor(cnt[:, :], run[:, :], iota_e[:, :], ALU.bypass).then_inc(ev("tb"), 1) if False else None
        V.scalar_tensor_tensor(out=cnt[:, :], in0=iota_e[:, :], scalar=-float(CAP), in1=run[:, :],
                               op0=ALU.mult, op1=ALU.add).then_inc(ev("counts"), 1)
        V.wait_ge(ev("counts"), 1)
        V.wait_ge(ev("w_cut"), T)
        V.tensor_tensor(over, cnt[:, :].unsqueeze(2).broadcast_to([P, E, T]),
                        thr[:, :].unsqueeze(1).broadcast_to([P, E, T]), ALU.is_gt).then_inc(ev("exceeds"), 1)
        V.wait_ge(ev("exceeds"), 1)
        V.tensor_reduce(nblk[:, :], over, AX_X, ALU.add).then_inc(ev("blocks"), 1)
        V.wait_ge(ev("blocks"), 1)
        V.tensor_tensor(tmp3, tri[:, :, :], nblk[:, :].unsqueeze(1).broadcast_to([P, E, E]), ALU.mult)\
         .then_inc(ev("blocks_tri"), 1)
        V.wait_ge(ev("blocks_tri"), 1)
        V.tensor_reduce(cum[:, :], tmp3, AX_X, ALU.add).then_inc(ev("blocks_cum"), 1)
        V.wait_ge(ev("blocks_cum"), 1)
        V.tensor_scalar(cum[:, :], cum[:, :], iota_p[:, 0:1], None, ALU.is_le).then_inc(ev("passed"), 1)
        V.wait_ge(ev("passed"), 1)
        V.tensor_reduce(tbl[:, 0:1], cum[:, :], AX_X, ALU.add).then_inc(ev("expert"), 1)
        V.tensor_tensor_reduce(out=junk[:, 0, :], in0=cum[:, :], in1=nblk[:, :], scale=1.0, scalar=0.0,
                               op0=ALU.mult, op1=ALU.add, accum_out=tbl[:, 1:2]).then_inc(ev("start"), 1)
        V.wait_ge(ev("start"), 1)
        V.tensor_scalar(tbl[:, 2:3], iota_p[:, 0:1], tbl[:, 1:2], float(P), ALU.subtract, ALU.mult)\
         .then_inc(ev("offset"), 1)
        V.wait_ge(ev("offset"), 1)
        V.wait_ge(ev("expert"), 1)
        V.scalar_tensor_tensor(out=tbl[:, 3:4], in0=tbl[:, 0:1], scalar=float(CAP), in1=tbl[:, 2:3],
                               op0=ALU.mult, op1=ALU.add).then_inc(ev("row"), 1)
        V.tensor_scalar(tabi[:, 1:2], tbl[:, 0:1], float(E - 1), None, ALU.min).then_inc(ev("expert_put"), 1)
        V.wait_ge(ev("row"), 1)
        V.wait_ge(ev("expert_put"), 1)
        V.tensor_copy(tabi[:, 0:1], tbl[:, 3:4]).then_inc(ev("table_made"), 1)

        V.wait_ge(ev("table_in"), 16)
        V.wait_ge(ev("b1_in"), 16)

        def copy_tokens_T(q, r):
            after(V, "tokens_T", blk(q, r))
            if not isinstance(q, int) or blk(q, r) >= 2:
                after(V, "hidden", blk(q, r) - 2)
            V.tensor_copy(xgT[:, r % 2, :], q_x[r % 2][:, 0:2 * D]).then_inc(ev("tokens_T_copied"), 1)

        def bias1(q, r):
            e = V.value_load(tab[0:1, bass.ds(blk(q, r) * 2 + 1, 1)], min_val=0, max_val=E - 1)
            after(V, "hidden", blk(q, r))
            if not isinstance(q, int) or blk(q, r) >= 2:
                after(V, "gelued", blk(q, r) - 2)
            V.scalar_tensor_tensor(out=hb[r % 2], in0=q_h[r % 2][:, :], scalar=1.0 / (SX * SW),
                                   in1=b1all[:, bass.ds(e * H, H)],
                                   op0=ALU.mult, op1=ALU.add).then_inc(ev("biased"), 1)

        def cut_low(q, r):
            after(V, "high_cut", blk(q, r))
            V.scalar_tensor_tensor(out=hl[:, r % 2, :], in0=q_g[r % 2][:, :], scalar=SH, in1=hh[:, r % 2, :],
                                   op0=ALU.mult, op1=ALU.subtract).then_inc(ev("low_cut"), 1)

        copy_tokens_T(0, 0)

        def bstep(q, r):
            prev, nxt = shift(q, r, -1), shift(q, r, 1)
            if exists(*prev):
                cut_low(*prev)
            if exists(q, r):
                bias1(q, r)
            if exists(*nxt):
                copy_tokens_T(*nxt)

        over_blocks(V, bstep)

    @block.gpsimd
    def _(pool):
        L = pool
        L.memset(ones16[:, :], 1.0).then_inc(ev("p_ones16"), 1)
        L.memset(id32[:, :], 0.0).then_inc(ev("p_id32"), 1)
        L.wait_ge(ev("p_id32"), 1)
        L.affine_select(out=id32[:, :], in_=id32[:, :], compare_op=ALU.not_equal, fill=1.0, base=0,
                        pattern=[[-1, P]], channel_multiplier=1).then_inc(ev("p_id32"), 1)
        L.wait_ge(ev("p_id32"), 2)
        L.tensor_copy(id16[:, :], id32[:, :]).then_inc(ev("p_id16"), 1)
        L.wait_ge(ev("p_ones16"), 1)
        L.affine_select(out=before[:, :], in_=ones16[:, :], compare_op=ALU.is_gt, fill=0.0, base=0,
                        pattern=[[1, P]], channel_multiplier=-1).then_inc(ev("p_before"), 1)
        L.iota(iota_e[:, :], [[1, E]], base=0, channel_multiplier=0, allow_small_or_imprecise_dtypes=True)\
         .then_inc(ev("p_iota_e"), 1)
        L.iota(iota_p[:, :], [[0, 1]], base=0, channel_multiplier=1, allow_small_or_imprecise_dtypes=True)\
         .then_inc(ev("p_iota_p"), 1)
        L.iota(tok[:, :], [[0, 1]], base=0, channel_multiplier=1, allow_small_or_imprecise_dtypes=True)\
         .then_inc(ev("p_tok"), 1)
        L.iota(run[:, :], [[CAP, E]], base=0, channel_multiplier=0, allow_small_or_imprecise_dtypes=True)\
         .then_inc(ev("p_run"), 1)
        L.iota(thr[:, :], [[P, T]], base=0, channel_multiplier=0, allow_small_or_imprecise_dtypes=True)\
         .then_inc(ev("p_thr"), 1)
        L.memset(mhalf[:, :], -0.5).then_inc(ev("p_mhalf"), 1)
        L.memset(place[:, :, :], 0).then_inc(ev("p_place"), 1)
        L.memset(tri[:, :, :], 1.0).then_inc(ev("p_tri"), 1)
        L.wait_ge(ev("p_tri"), 1)
        L.affine_select(out=tri[:, :, :], in_=tri[:, :, :], compare_op=ALU.is_ge, fill=0.0, base=0,
                        pattern=[[1, E], [-1, E]], channel_multiplier=0).then_inc(ev("ids_made"), 1)
        L.wait_ge(ev("p_mhalf"), 1)

        def rstd0(c):
            after(L, "var_ready", c)
            L.tensor_tensor(rstd[:, c * XT:(c + 1) * XT], var8[:, c, :], mhalf[:, :], ALU.pow)\
             .then_inc(ev("rstd_made"), 1)

        def low0(c):
            after(L, "xh_made", c)
            src = (xin if c < 2 else xin2)[:, (c % 2) * XT:(c % 2 + 1) * XT, :]
            L.tensor_tensor(xl[:, c * XT:(c + 1) * XT, :], src, xh[:, c * XT:(c + 1) * XT, 0:D], ALU.subtract)\
             .then_inc(ev("xparts_made"), 1)

        rstd0(0)
        for c in range(XC):
            if c + 1 < XC:
                rstd0(c + 1)
            low0(c)

        L.memset(pads[:, :, :], 0).then_inc(ev("pads_zero"), 1)
        L.memset(pads2[:, :, :], 0).then_inc(ev("pads_zero"), 1)
        L.wait_ge(ev("pads_zero"), 2)
        Q = E * CAP // P
        L.iota(pads[:, :, 0], [[0, Q // P], [1, P]], base=N, channel_multiplier=0).then_inc(ev("pads_made"), 1)
        L.iota(pads2[:, :, 0], [[0, SPARE]], base=N, channel_multiplier=1).then_inc(ev("pads_made"), 1)
        L.wait_ge(ev("pads_made"), 2)
        L.dma_start(lists[0:E * CAP, :].rearrange("(p q) w -> p q w", q=Q), pads).then_inc(ev("lists_filled"), 16)
        L.dma_start(lists[E * CAP:PLACES, :].rearrange("(q p) w -> p q w", p=P), pads2)\
         .then_inc(ev("lists_filled"), 16)
        L.wait_ge(ev("zeros_made"), 1)
        L.dma_start(total[N:N + P, :], zrow[:, :]).then_inc(ev("spare_rows"), 16)
        L.dma_start(feats[N:N + P, :], zrow[:, :].bitcast(F16)).then_inc(ev("spare_rows"), 16)
        L.wait_ge(ev("lists_filled"), 32)
        L.wait_ge(ev("ones_made"), 1)
        L.wait_ge(ev("xparts_made"), XC)

        def cut_weights(t, odd, e):
            L.wait_ge(ev("w_in"), t * 16 + 16)
            passed(L, "w_in")
            high, low = ((w1h, w1l), (w2h, w2l))[odd]
            n = DC * H
            L.tensor_scalar(wst[:, :], wst[:, :], SW, None, ALU.mult).then_inc(ev("w_scaled"), 1)
            after(L, "w_scaled", t)
            L.tensor_copy(high[:, bass.ds(e * n, n)], wst[:, :]).then_inc(ev("w_high"), 1)
            after(L, "w_high", t)
            L.tensor_tensor(low[:, bass.ds(e * n, n)], wst[:, :], high[:, bass.ds(e * n, n)], ALU.subtract)\
             .then_inc(ev("w_cut"), 1)

        def rstd1(s):
            after(L, "x1_var", s)
            L.tensor_tensor(vr[:, 1:2], vr[:, 0:1], mhalf[:, 0:1], ALU.pow).then_inc(ev("x1_rstd"), 1)

        def store_feats(s):
            after(L, "high_made", s)
            L.tensor_tensor(pay[:, D:2 * D], xf[:, :], pay[:, 0:D], ALU.subtract).then_inc(ev("low_made"), 1)
            after(L, "low_made", s)
            L.dma_start(feats[bass.ds(s * P, P), :], pay[:, :]).then_inc(ev("feats_out"), 16)

        def list_tokens(s):
            after(L, "placed", s)
            after(L, "token_put", s)
            after(L, "weight_put", s)
            passed(L, "placed")
            for k in range(TOPK):
                L.indirect_dma_start(lists, bass.IndirectOffsetOnAxis(ap=posi[:, k:k + 1].bitcast(U32), axis=0),
                                     place[:, k, :], None).then_inc(ev("listed"), 16)

        def store_base(s, odd):
            after(L, "base_made", s)
            L.dma_start(total[bass.ds(s * P, P), :], base[:, odd, :]).then_inc(ev("total_out"), 16)

        def step(t, odd, e):
            s, r = t - 1, t - 2
            if is_(t, lambda t: t < T):
                cut_weights(t, odd, e)
            if is_(s, lambda s: 0 <= s < T):
                rstd1(s)
            if is_(r, lambda r: 0 <= r < T):
                list_tokens(r)
            if is_(s, lambda s: 0 <= s < T):
                store_feats(s)
            if is_(r, lambda r: 0 <= r < T):
                store_base(r, odd)

        for t in (0, 1):
            step(t, t, 0)
        with L.Fori(1, T // 2 - 1) as i:
            step(i * 2, 0, i)
            step(i * 2 + 1, 1, i)
        for t in range(T - 2, T + 2):
            step(t, t % 2, t // 2)

        L.wait_ge(ev("feats_out"), 16 * T)
        L.wait_ge(ev("total_out"), 16 * T)
        L.wait_ge(ev("spare_rows"), 32)

        def gather(q, r):
            landed(L, lst_in, q, r)
            if not isinstance(q, int) or q >= 1:
                after(L, "tokens_T", blk(q, r) - 4)
            passed(L, "lst_in")
            L.indirect_dma_start(xg[r], None, feats,
                                 bass.IndirectOffsetOnAxis(ap=info[:, r, 0:1].bitcast(U32), axis=0))\
             .then_inc(xg_in[r], 16)

        def add_rows(q, r):
            after(L, "weighted", blk(q, r))
            if not isinstance(q, int) or blk(q, r) >= 1:
                landed(L, added, *shift(q, r, -1))
            passed(L, "weighted")
            L.indirect_dma_start(total, bass.IndirectOffsetOnAxis(ap=info[:, r, 0:1].bitcast(U32), axis=0),
                                 orow[r], None, compute_op=ALU.add).then_inc(added[r], 16)

        for r in range(2):
            gather(0, r)

        def bstep(q, r):
            nxt, prev = shift(q, r, 2), shift(q, r, -1)
            if exists(*nxt):
                gather(*nxt)
            if exists(*prev):
                add_rows(*prev)

        over_blocks(L, bstep)

    ctx.close()


_INS = ['x', 'adj', 'L0_gnn_W', 'L0_gnn_b', 'L0_ffn_Wr', 'L0_ffn_br', 'L0_ffn_W1', 'L0_ffn_b1', 'L0_ffn_W2', 'L0_ffn_b2']
_OUTS = [((N, D), 'float32')]


def kernel(**inputs):
    import numpy as _np
    import concourse.bacc as _bacc
    from concourse import mybir as _mybir
    from concourse.bass_utils import run_bass_kernel_spmd as _run

    nc = _bacc.Bacc("TRN2", target_bir_lowering=False, num_devices=1)
    arrays, args = {}, []
    for name in _INS:
        a = _np.ascontiguousarray(inputs[name])
        arrays[f"in_{name}_dram"] = a
        args.append(nc.dram_tensor(f"in_{name}_dram", a.shape, _mybir.dt.from_np(a.dtype), kind="ExternalInput").ap())
    for i, (shape, dtype) in enumerate(_OUTS):
        dt = _mybir.dt.from_np(_np.dtype(dtype))
        args.append(nc.dram_tensor(f"out_{i}_dram", shape, dt, kind="ExternalOutput").ap())
    build(nc, *args)
    r = _run(nc, [arrays], core_ids=[0])
    got = tuple(r.results[0][f"out_{i}_dram"] for i in range(len(_OUTS)))
    return got[0]
```

```python
from contextlib import ExitStack

import numpy as np

import concourse.bass as bass
from concourse import mybir

ALU = mybir.AluOpType
ACT = mybir.ActivationFunctionType
AX_X = mybir.AxisListType.X
F32 = mybir.dt.float32
F16 = mybir.dt.float16
I32 = mybir.dt.int32
U32 = mybir.dt.uint32

P = 128
N = 4096
D = 256
E = 16
H = 512
TOPK = 2
T = N // P
DC = D // P
HC = H // P
CH = 4
CW = N // CH
JC = CW // P
G = 2 * CH
XC = CH
XT = T // XC
HW = D + 2
EPS = 1e-5

CAP = N
BLOCKS = N * TOPK // P + E - 1
U = 8
ROUNDS = (BLOCKS + U - 1) // U
SPARE = ROUNDS * U - N * TOPK // P
PLACES = E * CAP + SPARE * P
LW = 16

SX = 2.0 ** 11
SW = 2.0 ** 8
SH = 2.0 ** 6


def build(nc, x, adj, gnn_W, gnn_b, Wr, br, W1, b1, W2, b2, out):
    ctx = ExitStack()

    def sb(name, shape, dt):
        return ctx.enter_context(nc.sbuf_tensor(name, shape, dt))

    def sem(name):
        return ctx.enter_context(nc.semaphore(name))

    feats = nc.dram_tensor("feats", (N + P, 2 * D), F32, kind="Internal").ap()
    lists = nc.dram_tensor("lists", (PLACES, LW), I32, kind="Internal").ap()
    results = nc.dram_tensor("results", (TOPK * N + P, D), F32, kind="Internal").ap()

    w1h = sb("w1h", [P, E * DC * H], F16)
    w1l = sb("w1l", [P, E * DC * H], F16)
    w2h = sb("w2h", [P, E * HC * D], F16)
    w2l = sb("w2l", [P, E * HC * D], F16)
    xin = w2h[:, :].bitcast(F32).rearrange("p (n d) -> p n d", d=D)
    xin2 = w2l[:, :].bitcast(F32).rearrange("p (n d) -> p n d", d=D)
    pads = w1l[:, :].bitcast(I32).rearrange("p (q w) -> p q w", w=LW)
    pads2 = w1h[:, 0:SPARE * LW * 2].bitcast(I32).rearrange("p (q w) -> p q w", w=LW)
    xparts = sb("xparts", [P, T * (HW + D)], F16)
    xh = xparts[:, 0:T * HW].rearrange("p (n w) -> p n w", w=HW)
    xl = xparts[:, T * HW:T * (HW + D)].rearrange("p (n w) -> p n w", w=D)
    b1all = xparts[:, 0:2 * E * H].bitcast(F32)
    abuf = sb("abuf", [P, CH * CW], F32)
    xg = [abuf[:, k * 2 * D:(k + 1) * 2 * D] for k in range(4)]
    xg16 = [g[:, 0:D].bitcast(F16) for g in xg]
    hb = [abuf[:, 8 * D + k * H:8 * D + (k + 1) * H] for k in range(2)]
    hg = [abuf[:, 12 * D + k * H:12 * D + (k + 1) * H] for k in range(2)]
    a16 = sb("a16", [P, 2, CW], F16)
    at = sb("at", [P, 2, CW], F16)
    wst = sb("wst", [P, DC * H], F32)
    xgT, hh = at[:, :, 0:2 * D], at[:, :, 2 * D:2 * D + H]
    hl = sb("hl", [P, 2, H], F16)
    info = sb("info", [P, U, 3], I32)

    wg = sb("wg", [P, DC, D], F32)
    gb = sb("gb", [P, D], F32)
    wr = sb("wr", [P, DC, E], F32)
    brb = sb("brb", [P, E], F32)
    b2s = sb("b2s", [E, D], F32)
    id32 = sb("id32", [P, P], F32)
    id16 = sb("id16", [P, P], F16)
    before = sb("before", [P, P], F16)
    ones16 = sb("ones16", [P, P], F16)
    iota_e = sb("iota_e", [P, E], F32)
    iota_p = sb("iota_p", [P, 1], F32)
    thr = sb("thr", [P, T], F32)
    mhalf = sb("mhalf", [P, XT], F32)
    zrow = hl[:, :, :].rearrange("p a b -> p (a b)").bitcast(F32)

    mean = sb("mean", [P, T], F32)
    rstd = sb("rstd", [P, T], F32)
    st6 = sb("st6", [P, XC, XT, 6], F32)
    var8 = sb("var8", [P, XC, XT], F32)
    dif8 = sb("dif8", [P, XT], F32)

    xt = sb("xt", [P, 2, D], F32)
    xs = sb("xs", [P, D], F32)
    pooled = sb("pooled", [P, D], F32)
    eT = sb("eT", [P, D], F32)
    x1, xf = pooled, xs
    pay = sb("pay", [P, 2 * D], F16)
    base = sb("base", [P, 2, D], F32)
    orow = [xt[:, 0, :], xt[:, 1, :], eT[:, :], base[:, 0, :]]
    dinv2 = sb("dinv2", [P, 2], F32)
    bst = sb("bst", [P, 6], F32)
    mv = sb("mv", [P, 2], F32)
    vr = sb("vr", [P, 2], F32)
    lg = sb("lg", [P, E], F32)
    ex = sb("ex", [P, E], F32)
    pr = sb("pr", [P, E], F32)
    m8 = sb("m8", [P, 8], F32)
    p8 = sb("p8", [P, 8], F32)
    i8 = sb("i8", [P, 8], U32)
    sc = sb("sc", [P, 8], F32)
    i2 = sb("i2", [P, 2], F32)
    oh = sb("oh", [P, 2, E], F32)
    msk = sb("msk", [P, E], F16)
    cmb = sb("cmb", [P, E], F32)
    cT = sb("cT", [E, P], F32)
    run = sb("run", [P, E], F32)
    posb = sb("posb", [P, E], F32)
    junk = sb("junk", [P, 2, E], F32)
    posf = sb("posf", [P, 2], F32)
    posi = sb("posi", [P, 2], I32)
    tok = sb("tok", [P, TOPK, 2], F32)
    tok_step = sb("tok_step", [P, TOPK, 2], F32)
    place = sb("place", [P, 2, LW], I32)

    cnt = sb("cnt", [P, E], F32)
    nblk = sb("nblk", [P, E], F32)
    cum = sb("cum", [P, E], F32)
    tbl = sb("tbl", [P, 8], F32)
    tabi = sb("tabi", [P, 2], I32)
    tab = wst[0:1, E * T + E * E:E * T + E * E + 2 * P].bitcast(I32)
    over = wst[:, 0:E * T].rearrange("p (e m) -> p e m", m=T)
    tri = wst[:, E * T:E * T + E * E].rearrange("p (e f) -> p e f", f=E)
    tmp3 = wst[:, 0:E * E].rearrange("p (e f) -> p e f", f=E)

    banks = [ctx.enter_context(nc.psum_tensor(f"bank{i}", [P, 512], F32)) for i in range(8)]
    ps_tp = [b[:, :].bitcast(F16) for b in banks[0:2]]
    ps_acc = banks[2:4]
    ps_T, ps_Z, ps_S, ps_B = banks[4:8]
    q_x = [b[:, :].bitcast(F16) for b in banks[0:2]]
    q_h = banks[2:4]
    q_g = banks[4:6]
    q_o = banks[6:8]

    S = {}

    def ev(name):
        if name not in S:
            S[name] = sem(name)
        return S[name]

    def after(eng, name, t):
        eng.wait_ge(ev(name), t + 1)

    def passed(eng):
        eng.sem_inc(ev("passed"), 1)

    CONSTANTS = 16
    x_in = [sem(f"x_in{c}") for c in range(XC)]
    a_in = [sem(f"a_in{c}") for c in range(CH)]
    xt_in = [sem(f"xt_in{c}") for c in range(2)]
    lst_in = [sem(f"lst_in{c}") for c in range(U)]
    xg_in = [sem(f"xg_in{c}") for c in range(4)]
    stored = [sem(f"stored{c}") for c in range(4)]
    y_in = [sem(f"y_in{c}") for c in range(4)]
    y_out = [sem(f"y_out{c}") for c in range(4)]

    def landed4(eng, sems, q, r):
        eng.wait_ge(sems[r % 4], (q * (U // 4) + r // 4 + 1) * 16)

    def landed(eng, sems, q, r):
        eng.wait_ge(sems[r], (q + 1) * 16)

    FC = N // P // 4
    y_v = results[0:TOPK * N, :].rearrange("(p k j) d -> p k (j d)", p=P, k=FC)
    out_v = out.rearrange("(p k j) d -> p k (j d)", p=P, k=FC)
    ybuf = [w2h[:, :].bitcast(F32)[:, k * 8 * D:(k + 1) * 8 * D] for k in range(4)]
    obuf = [w2l[:, :].bitcast(F32)[:, k * 4 * D:(k + 1) * 4 * D] for k in range(4)]

    x_v = x.rearrange("(n p) d -> p n d", p=P)
    consts = [(wg[:, :, :], gnn_W.rearrange("(c p) n -> p c n", p=P)),
              (wr[:, :, :], Wr.rearrange("(c p) n -> p c n", p=P)),
              (b2s[:, :], b2),
              (gb[:, :], gnn_b.rearrange("(a d) -> a d", a=1).broadcast_to([P, D])),
              (brb[:, :], br.rearrange("(a d) -> a d", a=1).broadcast_to([P, E]))]

    def step_up(t, c, k):
        return t + (c + k) // CH, (c + k) % CH

    def over_tiles(eng, step):
        for t in (0, 1):
            step(t, t)
        with eng.Fori(1, T // 2 - 1) as i:
            step(i * 2, 0)
            step(i * 2 + 1, 1)
        for t in range(T - 2, T + 2):
            step(t, t % 2)

    def is_(t, cond):
        return cond(t) if isinstance(t, int) else True

    def over_blocks(eng, step):
        for r in range(U):
            step(0, r)
        with eng.Fori(1, ROUNDS - 1) as q:
            for r in range(U):
                step(q, r)
        for r in range(BLOCKS + 1 - U * (ROUNDS - 1)):
            step(ROUNDS - 1, r)

    def shift(q, r, k):
        return q + (r + k) // U, (r + k) % U

    def exists(q, r):
        return not isinstance(q, int) or 0 <= U * q + r < BLOCKS

    def blk(q, r):
        return q * U + r

    block = ctx.enter_context(nc.Block())

    @block.sync
    def _(sp):
        for dst, src in consts[0:2]:
            sp.dma_start(dst, src).then_inc(ev("consts_in"), 16)
        for c in range(XC):
            sp.dma_start(xin[:, c * XT:(c + 1) * XT, :] if c < 2 else xin2[:, (c - 2) * XT:(c - 1) * XT, :],
                         x_v[:, c * XT:(c + 1) * XT, :]).then_inc(x_in[c], 16)
            sp.dma_start(abuf[:, c * CW:(c + 1) * CW], adj[0:P, c * CW:(c + 1) * CW]).then_inc(a_in[c], 16)
        for dst, src in consts[2:]:
            sp.dma_start(dst, src).then_inc(ev("consts_in"), 16)

        def load_adj(t, c):
            sp.wait_ge(ev("cast"), t * CH - CH + c + 1)
            sp.dma_start(abuf[:, c * CW:(c + 1) * CW],
                         adj[bass.ds(t * P, P), c * CW:(c + 1) * CW]).then_inc(a_in[c], 16)

        def load_weights(t, odd):
            if is_(t, lambda t: t > 0):
                after(sp, "w_cut", t - 1)
            if odd:
                e = t // 2
                sp.dma_start(wst[:, :].rearrange("p (c n) -> p c n", c=HC),
                             W2[bass.ds(e, 1), :, :].rearrange("a (c p) n -> p (a c) n", p=P)).then_inc(ev("w_in"), 16)
            else:
                e = t // 2
                sp.dma_start(wst[:, :].rearrange("p (c n) -> p c n", c=DC),
                             W1[bass.ds(e, 1), :, :].rearrange("a (c p) n -> p (a c) n", p=P)).then_inc(ev("w_in"), 16)

        def step(t, odd):
            if is_(t, lambda t: t >= T):
                return
            if is_(t, lambda t: t > 0):
                for c in range(CH):
                    load_adj(t, c)
            if is_(t, lambda t: t >= 2):
                after(sp, "x1_made", t - 2)
            sp.dma_start(xt[:, odd, :], x[bass.ds(t * P, P), :]).then_inc(xt_in[odd], 16)
            load_weights(t, odd)

        def step_i(t, odd):
            step(t, odd)

        for t in (0, 1):
            step_i(t, t)
        with sp.Fori(1, T // 2) as i:
            for odd in (0, 1):
                t = i * 2 + odd
                for c in range(CH):
                    load_adj(t, c)
                after(sp, "x1_made", t - 2)
                sp.dma_start(xt[:, odd, :], x[bass.ds(t * P, P), :]).then_inc(xt_in[odd], 16)
                after(sp, "w_cut", t - 1)
                W, c = ((W1, DC), (W2, HC))[odd]
                sp.dma_start(wst[:, :].rearrange("p (c n) -> p c n", c=c),
                             W[bass.ds(i, 1), :, :].rearrange("a (c p) n -> p (a c) n", p=P)).then_inc(ev("w_in"), 16)

        sp.wait_ge(ev("multiplied"), T * CH)
        sp.dma_start(b1all, b1.rearrange("(a e) h -> a (e h)", a=1).broadcast_to([P, E * H])).then_inc(ev("b1_in"), 16)
        sp.wait_ge(ev("table_made"), 1)
        sp.dma_start(tab[0:1, :], tabi[:, :]).then_inc(ev("table_in"), 16)
        sp.wait_ge(ev("table_in"), 16)
        sp.wait_ge(ev("listed"), 16 * 2 * T)

        def load_list(q, r):
            if not isinstance(q, int) or q > 0:
                landed4(sp, stored, q - 1, r)
            row = sp.value_load(tab[0:1, bass.ds(blk(q, r) * 2, 1)], min_val=0, max_val=PLACES - P)
            sp.dma_start(info[:, r, :], lists[bass.ds(row, P), 0:3]).then_inc(lst_in[r], 16)

        for r in range(U):
            load_list(0, r)
        with sp.Fori(1, ROUNDS - 1) as q:
            for r in range(U):
                load_list(q, r)
        for r in range(BLOCKS - U * (ROUNDS - 1)):
            load_list(ROUNDS - 1, r)

        for n in range(BLOCKS - 4, BLOCKS):
            landed4(sp, stored, *divmod(n, U))
        after(sp, "expert_out", BLOCKS - 1)

        for k in range(FC):
            if k >= 4:
                after(sp, "summed", k - 4)
            sp.dma_start(ybuf[k % 4], y_v[:, k, :]).then_inc(y_in[k % 4], 16)
            if k >= 1:
                after(sp, "summed", k - 1)
                sp.dma_start(out_v[:, k - 1, :], obuf[(k - 1) % 4]).then_inc(y_out[(k - 1) % 4], 16)
        after(sp, "summed", FC - 1)
        sp.dma_start(out_v[:, FC - 1, :], obuf[(FC - 1) % 4]).then_inc(y_out[(FC - 1) % 4], 16)
        for k in range(4):
            sp.wait_ge(y_out[k], 16 * (FC // 4))

    @block.tensor
    def _(pe):
        def transposes(t, c):
            pe.wait_ge(ev("cast"), t * CH + c + 1)
            for j in range(JC):
                mm = pe.transpose(ps_tp[c % 2][:, j * P:(j + 1) * P], a16[:, c % 2, j * P:(j + 1) * P], id16[:, :])
            mm.then_inc(ev("transposed"), 1)

        def pooled_T(s):
            after(pe, "pooled", s)
            for c in range(DC):
                mm = pe.transpose(ps_T[:, c * P:(c + 1) * P], pooled[:, c * P:(c + 1) * P], id32[:, :])
            mm.then_inc(ev("pooled_T"), 1)

        def graph_out(s):
            after(pe, "pooled_T_copied", s)
            for c in range(DC):
                mm = pe.matmul(ps_Z[:, 0:D], eT[:, c * P:(c + 1) * P], wg[:, c, :], start=c == 0, stop=c == DC - 1)
            mm.then_inc(ev("graph_out"), 1)

        def xf_T(s):
            after(pe, "xf_made", s)
            for c in range(DC):
                mm = pe.transpose(ps_T[:, D + c * P:D + (c + 1) * P], xf[:, c * P:(c + 1) * P], id32[:, :])
            mm.then_inc(ev("xf_T"), 1)

        def logits(s):
            after(pe, "xf_T_copied", s)
            if is_(s, lambda s: s >= 1):
                after(pe, "run_counted", s - 1)
            for c in range(DC):
                mm = pe.matmul(ps_S[:, 0:E], eT[:, c * P:(c + 1) * P], wr[:, c, :], start=c == 0, stop=c == DC - 1)
            mm.then_inc(ev("logits"), 1)

        def rank(s):
            after(pe, "combine_made", s)
            pe.matmul(ps_S[:, E:2 * E], before[:, :], msk[:, :], start=True, stop=True)
            pe.matmul(ps_S[:, 2 * E:3 * E], ones16[:, :], msk[:, :], start=True, stop=True)
            if is_(s, lambda s: s >= 1):
                after(pe, "base_made", s - 1)
            pe.transpose(ps_B[0:E, D:D + P], cmb[:, :], id32[:, :]).then_inc(ev("ranked"), 1)

        def bias2(s):
            after(pe, "combine_T_copied", s)
            pe.matmul(ps_B[:, 0:D], cT[:, :], b2s[:, :], start=True, stop=True).then_inc(ev("bias2"), 1)

        def step(t, odd):
            s, r = t - 1, t - 2
            has_t = is_(t, lambda t: t < T)
            has_s = is_(s, lambda s: 0 <= s < T)
            has_r = is_(r, lambda r: 0 <= r < T)
            for g in range(G):
                c, half = divmod(g, 2)
                if has_t and not half:
                    pe.wait_ge(ev("at_made"), t * CH + c + 1)
                    t2, c2 = step_up(t, c, 2)
                    if is_(t2, lambda t2: t2 < T):
                        transposes(t2, c2)
                    if c == 0 and is_(t, lambda t: t >= 2):
                        after(pe, "acc_read", t - 2)
                    if isinstance(t, int) and t == 0:
                        after(pe, "xparts_made", c)
                if has_t:
                    for j in range(g * JC // 2, (g + 1) * JC // 2):
                        w = at[:, c % 2, (j % JC) * P:(j % JC + 1) * P]
                        both = [lambda: pe.matmul(ps_acc[odd][:, 0:D + 1], w, xh[:, j, 0:D + 1],
                                                  start=j == 0, stop=j == T - 1),
                                lambda: pe.matmul(ps_acc[odd][:, 0:D], w, xl[:, j, :], start=False, stop=False)]
                        if j == T - 1:
                            both.reverse()
                        for product in both:
                            mm = product()
                    if half:
                        mm.then_inc(ev("multiplied"), 1)
                if g == 0 and has_r:
                    logits(r)
                if g == 1 and has_s:
                    pooled_T(s)
                if g == 3 and has_s:
                    graph_out(s)
                if g == 4 and has_r:
                    rank(r)
                if g == 6 and has_r:
                    bias2(r)
                if g == 7 and has_s:
                    xf_T(s)

        pe.wait_ge(ev("constants"), CONSTANTS)
        transposes(0, 0)
        transposes(0, 1)
        pe.wait_ge(ev("consts_in"), 16 * len(consts))
        over_tiles(pe, step)

        def tokens_T(q, r):
            landed4(pe, xg_in, q, r)
            if not isinstance(q, int) or blk(q, r) >= 2:
                after(pe, "tokens_T_copied", blk(q, r) - 2)
            for c in range(2 * DC):
                mm = pe.transpose(q_x[r % 2][:, c * P:(c + 1) * P], xg16[r % 4][:, c * P:(c + 1) * P], id16[:, :])
            mm.then_inc(ev("tokens_T"), 1)

        def hidden(q, r):
            after(pe, "tokens_T_copied", blk(q, r))
            if not isinstance(q, int) or blk(q, r) >= 2:
                after(pe, "biased", blk(q, r) - 2)
            passed(pe)
            e = pe.value_load(tab[0:1, bass.ds(blk(q, r) * 2 + 1, 1)], min_val=0, max_val=E - 1)
            n = 0
            for c in range(DC):
                high = xgT[:, r % 2, c * P:(c + 1) * P]
                low = xgT[:, r % 2, D + c * P:D + (c + 1) * P]
                wh = w1h[:, bass.ds(e * (DC * H) + c * H, H)]
                wl = w1l[:, bass.ds(e * (DC * H) + c * H, H)]
                for a, w in ((high, wh), (high, wl), (low, wh)):
                    mm = pe.matmul(q_h[r % 2][:, :], a, w, start=n == 0, stop=n == 3 * DC - 1)
                    n += 1
            mm.then_inc(ev("hidden"), 1)

        def hidden_T(q, r):
            after(pe, "gelued", blk(q, r))
            if not isinstance(q, int) or blk(q, r) >= 2:
                after(pe, "low_cut", blk(q, r) - 2)
            for c in range(HC):
                mm = pe.transpose(q_g[r % 2][:, c * P:(c + 1) * P], hg[r % 2][:, c * P:(c + 1) * P], id32[:, :])
            mm.then_inc(ev("hidden_T"), 1)

        def expert_out(q, r):
            after(pe, "low_cut", blk(q, r))
            if not isinstance(q, int) or blk(q, r) >= 2:
                after(pe, "weighted", blk(q, r) - 2)
            passed(pe)
            e = pe.value_load(tab[0:1, bass.ds(blk(q, r) * 2 + 1, 1)], min_val=0, max_val=E - 1)
            n = 0
            for c in range(HC):
                high, low = hh[:, r % 2, c * P:(c + 1) * P], hl[:, r % 2, c * P:(c + 1) * P]
                wh = w2h[:, bass.ds(e * (HC * D) + c * D, D)]
                wl = w2l[:, bass.ds(e * (HC * D) + c * D, D)]
                for a, w in ((high, wh), (high, wl), (low, wh)):
                    mm = pe.matmul(q_o[r % 2][:, 0:D], a, w, start=n == 0, stop=n == 3 * HC - 1)
                    n += 1
            mm.then_inc(ev("expert_out"), 1)

        pe.wait_ge(ev("table_in"), 16)
        after(pe, "base_made", T - 1)
        after(pe, "run_counted", T - 1)
        tokens_T(0, 0)

        def bstep(q, r):
            prev, nxt = shift(q, r, -1), shift(q, r, 1)
            if exists(*prev):
                hidden_T(*prev)
            if exists(q, r):
                hidden(q, r)
            if exists(*nxt):
                tokens_T(*nxt)
            if exists(*prev):
                expert_out(*prev)

        over_blocks(pe, bstep)

    @block.scalar
    def _(act):
        def cast(t, c):
            landed(act, a_in, t, c)
            if is_(t, lambda t: t * CH + c >= 2):
                act.wait_ge(ev("transposed"), t * CH + c - 1)
            act.activation(a16[:, c % 2, :], abuf[:, c * CW:(c + 1) * CW], ACT.Copy).then_inc(ev("cast"), 1)

        def cut_weights(t, odd, e):
            act.wait_ge(ev("w_in"), t * 16 + 16)
            n = DC * H
            act.activation((w1h, w2h)[odd][:, bass.ds(e * n, n)], wst[:, :], ACT.Copy, scale=SW)\
               .then_inc(ev("w_high"), 1)
            after(act, "w_high", t)
            act.activation(wst[:, :], wst[:, :], ACT.Copy, scale=SW).then_inc(ev("w_scaled"), 1)

        def copy_pooled_T(s):
            after(act, "pooled_T", s)
            if is_(s, lambda s: s >= 1):
                after(act, "logits", s - 1)
            act.activation(eT[:, :], ps_T[:, 0:D], ACT.Copy).then_inc(ev("pooled_T_copied"), 1)

        def copy_xf_T(s):
            after(act, "xf_T", s)
            act.activation(eT[:, :], ps_T[:, D:2 * D], ACT.Copy).then_inc(ev("xf_T_copied"), 1)

        def high_part(s):
            after(act, "xf_made", s)
            if is_(s, lambda s: s >= 1):
                after(act, "feats_out", s * 16 - 1)
            act.activation(pay[:, 0:D], xf[:, :], ACT.Copy).then_inc(ev("high_made"), 1)

        def exps(s):
            after(act, "max_made", s)
            act.activation(ex[:, :], lg[:, :], ACT.Exp, bias=sc[:, 0:1], accum_out=sc[:, 1:2])\
               .then_inc(ev("exps_made"), 1)

        def copy_combine_T(s):
            after(act, "ranked", s)
            if is_(s, lambda s: s >= 1):
                after(act, "bias2", s - 1)
            act.activation(cT[:, :], ps_B[0:E, D:D + P], ACT.Copy, scale=0.5).then_inc(ev("combine_T_copied"), 1)

        cast(0, 0)
        cast(0, 1)
        for c in range(XC):
            after(act, "x_scaled", c)
            src = (xin if c < 2 else xin2)[:, (c % 2) * XT:(c % 2 + 1) * XT, :]
            act.activation(xh[:, c * XT:(c + 1) * XT, 0:D], src, ACT.Copy).then_inc(ev("xh_made"), 1)
            if c == 0:
                cast(0, 2)
        act.wait_ge(ev("lists_filled"), 32)
        act.wait_ge(ev("xparts_made"), XC)

        def step(t, odd, e):
            s, r = t - 1, t - 2
            has_s = is_(s, lambda s: 0 <= s < T)
            has_r = is_(r, lambda r: 0 <= r < T)
            for g in range(G):
                if g == 0 and has_r:
                    copy_xf_T(r)
                if g % 2 == 0:
                    t2, c2 = step_up(t, g // 2, 3)
                    if is_(t2, lambda t2: t2 < T):
                        cast(t2, c2)
                if g == 1 and has_r:
                    exps(r)
                if g == 2 and has_s:
                    copy_pooled_T(s)
                if g == 3 and is_(t, lambda t: t < T):
                    cut_weights(t, odd, e)
                if g == 5 and has_r:
                    copy_combine_T(r)
                if g == 7 and has_s:
                    high_part(s)

        for t in (0, 1):
            step(t, t, 0)
        with act.Fori(1, T // 2 - 1) as i:
            step(i * 2, 0, i)
            step(i * 2 + 1, 1, i)
        for t in range(T - 2, T + 2):
            step(t, t % 2, t // 2)

        def gelu(q, r):
            after(act, "biased", blk(q, r))
            if not isinstance(q, int) or blk(q, r) >= 2:
                after(act, "hidden_T", blk(q, r) - 2)
            act.activation(hg[r % 2], hb[r % 2], ACT.Gelu).then_inc(ev("gelued"), 1)

        def cut_high(q, r):
            after(act, "hidden_T", blk(q, r))
            if not isinstance(q, int) or blk(q, r) >= 2:
                after(act, "expert_out", blk(q, r) - 2)
            act.activation(hh[:, r % 2, :], q_g[r % 2][:, :], ACT.Copy, scale=SH).then_inc(ev("high_cut"), 1)

        def bstep(q, r):
            prev = shift(q, r, -1)
            if exists(*prev):
                cut_high(*prev)
            if exists(q, r):
                gelu(q, r)

        over_blocks(act, bstep)

    @block.vector
    def _(dve):
        V = dve

        def tile_of(c):
            return (xin if c < 2 else xin2), (c % 2) * XT

        def stats(c):
            src, k0 = tile_of(c)
            V.wait_ge(x_in[c], 16)
            for k in range(XT):
                last = V.bn_stats(st6[:, c, k, :], src[:, k + k0, :])
            last.then_inc(ev("bn"), 1)
            after(V, "bn", c)
            m_e, m_o = st6[:, c, :, 1], st6[:, c, :, 4]
            v_e, v_o = st6[:, c, :, 2], st6[:, c, :, 5]
            V.tensor_tensor(mean[:, c * XT:(c + 1) * XT], m_e, m_o, ALU.add).then_inc(ev("mean_sum"), 1)
            V.tensor_tensor(dif8[:, :], m_e, m_o, ALU.subtract).then_inc(ev("dif"), 1)
            V.tensor_tensor(var8[:, c, :], v_e, v_o, ALU.add).then_inc(ev("var_sum"), 1)
            after(V, "mean_sum", c)
            V.tensor_scalar(mean[:, c * XT:(c + 1) * XT], mean[:, c * XT:(c + 1) * XT], 0.5, None, ALU.mult)\
             .then_inc(ev("mean_made"), 1)
            after(V, "dif", c)
            V.tensor_tensor(dif8[:, :], dif8[:, :], dif8[:, :], ALU.mult).then_inc(ev("dif2"), 1)
            after(V, "dif2", c)
            after(V, "var_sum", c)
            V.scalar_tensor_tensor(out=var8[:, c, :], in0=dif8[:, :], scalar=D / 4.0, in1=var8[:, c, :],
                                   op0=ALU.mult, op1=ALU.add).then_inc(ev("var_made"), 1)
            after(V, "var_made", c)
            V.tensor_scalar(var8[:, c, :], var8[:, c, :], 1.0 / D, EPS, ALU.mult, ALU.add)\
             .then_inc(ev("var_eps"), 1)
            after(V, "var_eps", c)
            V.tensor_scalar(var8[:, c, :], var8[:, c, :], SX ** -2, None, ALU.mult).then_inc(ev("var_ready"), 1)

        def scale_x(c):
            src, k0 = tile_of(c)
            after(V, "rstd_made", c)
            after(V, "mean_made", c)
            for k in range(XT):
                last = V.tensor_scalar(src[:, k + k0, :], src[:, k + k0, :], mean[:, c * XT + k:c * XT + k + 1],
                                       rstd[:, c * XT + k:c * XT + k + 1], ALU.subtract, ALU.mult)
            last.then_inc(ev("x_scaled"), 1)

        V.memset(zrow, 0.0).then_inc(ev("zeros_made"), 1)
        V.memset(xh[:, :, D:D + 2], 1.0).then_inc(ev("ones_made"), 1)

        def copy_chunk(t, c):
            V.wait_ge(ev("transposed"), t * CH + c + 1)
            if is_(t, lambda t: t * CH + c >= 2):
                V.wait_ge(ev("multiplied"), t * CH + c - 1)
            V.tensor_copy(at[:, c % 2, :], ps_tp[c % 2]).then_inc(ev("at_made"), 1)

        stats(0)
        copy_chunk(0, 0)
        for c in range(XC):
            if c + 1 < XC:
                stats(c + 1)
            scale_x(c)
        copy_chunk(0, 1)

        def pool_x(s, odd):
            V.wait_ge(xt_in[odd], s // 2 * 16 + 16 if isinstance(s, int) else (s - odd) * 8 + 16)
            if is_(s, lambda s: s >= 1):
                after(V, "xf_T", s - 1)
                after(V, "high_made", s - 1)
                after(V, "low_made", s - 1)
                after(V, "residual_made", s - 1)
            V.tensor_scalar(xs[:, :], xt[:, odd, :], mean[:, bass.ds(s, 1)], rstd[:, bass.ds(s, 1)],
                            ALU.subtract, ALU.mult).then_inc(ev("xs_made"), 1)
            V.wait_ge(ev("multiplied"), s * CH + CH)
            V.tensor_scalar(dinv2[:, 0:1], ps_acc[odd][:, D:D + 1], 1.0, None, ALU.max).then_inc(ev("degree"), 1)
            after(V, "degree", s)
            V.reciprocal(dinv2[:, 1:2], dinv2[:, 0:1]).then_inc(ev("dinv2"), 1)
            after(V, "xs_made", s)
            V.tensor_tensor(pooled[:, :], ps_acc[odd][:, 0:D], xs[:, :], ALU.add).then_inc(ev("acc_read"), 1)
            after(V, "acc_read", s)
            after(V, "dinv2", s)
            V.scalar_tensor_tensor(out=pooled[:, :], in0=pooled[:, :], scalar=dinv2[:, 1:2], in1=xs[:, :],
                                   op0=ALU.mult, op1=ALU.add).then_inc(ev("pooled"), 1)

        def graph_add(s, odd):
            after(V, "graph_out", s)
            V.scalar_tensor_tensor(out=x1[:, :], in0=ps_Z[:, 0:D], scalar=1.0 / SX, in1=gb[:, :],
                                   op0=ALU.mult, op1=ALU.add).then_inc(ev("graph_biased"), 1)
            after(V, "graph_biased", s)
            V.scalar_tensor_tensor(out=x1[:, :], in0=x1[:, :], scalar=0.0, in1=xt[:, odd, :],
                                   op0=ALU.max, op1=ALU.add).then_inc(ev("x1_made"), 1)
            after(V, "x1_made", s)
            V.bn_stats(bst[:, :], x1[:, :]).then_inc(ev("x1_stats"), 1)
            after(V, "x1_stats", s)
            passed(V)
            V.bn_aggr(mv[:, :], bst[:, :]).then_inc(ev("x1_aggr"), 1)
            after(V, "x1_aggr", s)
            V.tensor_scalar(vr[:, 0:1], mv[:, 1:2], EPS, SX ** -2, ALU.add, ALU.mult).then_inc(ev("x1_var"), 1)

        def norm_x1(s, odd):
            after(V, "x1_rstd", s)
            V.tensor_scalar(xf[:, :], x1[:, :], mv[:, 0:1], vr[:, 1:2], ALU.subtract, ALU.mult)\
             .then_inc(ev("xf_made"), 1)
            after(V, "xf_made", s)
            if is_(s, lambda s: s >= 2):
                V.wait_ge(ev("base_out"), (s - 1) * 16)
            V.scalar_tensor_tensor(out=base[:, odd, :], in0=xf[:, :], scalar=1.0 / SX, in1=x1[:, :],
                                   op0=ALU.mult, op1=ALU.add).then_inc(ev("residual_made"), 1)

        def top1(s):
            after(V, "logits", s)
            V.scalar_tensor_tensor(out=lg[:, :], in0=ps_S[:, 0:E], scalar=1.0 / SX, in1=brb[:, :],
                                   op0=ALU.mult, op1=ALU.add).then_inc(ev("lg_made"), 1)
            after(V, "lg_made", s)
            V.tensor_reduce(m8[:, 0:1], lg[:, :], AX_X, ALU.max).then_inc(ev("max_found"), 1)
            after(V, "max_found", s)
            V.tensor_scalar(sc[:, 0:1], m8[:, 0:1], -1.0, None, ALU.mult).then_inc(ev("max_made"), 1)

        def top2(s):
            after(V, "exps_made", s)
            V.reciprocal(sc[:, 2:3], sc[:, 1:2]).then_inc(ev("sum_inv"), 1)
            after(V, "sum_inv", s)
            V.tensor_scalar(pr[:, :], ex[:, :], sc[:, 2:3], None, ALU.mult).then_inc(ev("probs"), 1)
            after(V, "probs", s)
            passed(V)
            V.max(p8[:, :], pr[:, :]).then_inc(ev("top_p"), 1)
            after(V, "top_p", s)
            passed(V)
            V.max_index(i8[:, :], p8[:, :], pr[:, :]).then_inc(ev("top_i"), 1)
            V.tensor_scalar(sc[:, 3:4], p8[:, 0:1], p8[:, 1:2], 1e-9, ALU.add, ALU.max).then_inc(ev("top_sum"), 1)
            after(V, "top_sum", s)
            V.reciprocal(sc[:, 4:5], sc[:, 3:4]).then_inc(ev("top_inv"), 1)
            after(V, "top_i", s)
            V.tensor_copy(i2[:, :], i8[:, 0:2]).then_inc(ev("top_if"), 1)
            after(V, "top_inv", s)
            V.tensor_scalar(sc[:, 5:7], p8[:, 0:2], sc[:, 4:5], None, ALU.mult).then_inc(ev("top_w"), 1)
            after(V, "top_if", s)
            V.tensor_scalar(oh[:, 0, :], iota_e[:, :], i2[:, 0:1], None, ALU.is_equal).then_inc(ev("hot0"), 1)
            V.tensor_scalar(oh[:, 1, :], iota_e[:, :], i2[:, 1:2], None, ALU.is_equal).then_inc(ev("hot1"), 1)
            after(V, "hot1", s)
            after(V, "hot0", s)
            V.tensor_tensor(msk[:, :], oh[:, 0, :], oh[:, 1, :], ALU.add).then_inc(ev("mask_made"), 1)
            after(V, "top_w", s)
            V.tensor_scalar(cmb[:, :], oh[:, 0, :], sc[:, 5:6], None, ALU.mult).then_inc(ev("combine0"), 1)
            after(V, "combine0", s)
            V.scalar_tensor_tensor(out=cmb[:, :], in0=oh[:, 1, :], scalar=sc[:, 6:7], in1=cmb[:, :],
                                   op0=ALU.mult, op1=ALU.add).then_inc(ev("combine_made"), 1)

        def places(s):
            after(V, "ranked", s)
            V.tensor_tensor(posb[:, :], ps_S[:, E:2 * E], run[:, :], ALU.add).then_inc(ev("place_base"), 1)
            after(V, "place_base", s)
            V.tensor_tensor(run[:, :], ps_S[:, 2 * E:3 * E], run[:, :], ALU.add).then_inc(ev("run_counted"), 1)
            for k in range(TOPK):
                V.tensor_tensor_reduce(out=junk[:, k, :], in0=posb[:, :], in1=oh[:, k, :], scale=1.0, scalar=0.0,
                                       op0=ALU.mult, op1=ALU.add, accum_out=posf[:, k:k + 1])\
                 .then_inc(ev(f"place{k}"), 1)
            if is_(s, lambda s: s >= 1):
                after(V, "listed", s * 32 - 1)
                after(V, "token_next", s - 1)
            V.tensor_copy(place[:, :, 0:2], tok[:, :, :]).then_inc(ev("rows_put"), 1)
            V.tensor_scalar(place[:, :, 2].bitcast(F32), sc[:, 5:7], 1.0 / (SH * SW), None, ALU.mult)\
             .then_inc(ev("weight_put"), 1)
            after(V, "place0", s)
            after(V, "place1", s)
            V.tensor_copy(posi[:, :], posf[:, :]).then_inc(ev("placed"), 1)
            after(V, "rows_put", s)
            V.tensor_tensor(tok[:, :, :], tok[:, :, :], tok_step[:, :, :], ALU.add).then_inc(ev("token_next"), 1)

        def finish_base(s, odd):
            after(V, "bias2", s)
            after(V, "residual_made", s)
            V.scalar_tensor_tensor(out=base[:, odd, :], in0=base[:, odd, :], scalar=0.5, in1=ps_B[:, 0:D],
                                   op0=ALU.mult, op1=ALU.add).then_inc(ev("base_made"), 1)

        V.wait_ge(ev("constants"), CONSTANTS)
        V.wait_ge(ev("consts_in"), 16 * len(consts))

        def step(t, odd):
            s, r = t - 1, t - 2
            has_s = is_(s, lambda s: 0 <= s < T)
            has_r = is_(r, lambda r: 0 <= r < T)
            for g in range(G):
                if g % 2 == 0:
                    t2, c2 = step_up(t, g // 2, 1)
                    if is_(t2, lambda t2: t2 < T and (t2, c2) != (0, 1)):
                        copy_chunk(t2, c2)
                if g == 0 and has_s:
                    pool_x(s, 1 - odd)
                if g == 1 and has_r:
                    top1(r)
                if g == 2 and has_r:
                    top2(r)
                if g == 4 and has_s:
                    graph_add(s, 1 - odd)
                if g == 5 and has_r:
                    places(r)
                if g == 6 and has_s:
                    norm_x1(s, 1 - odd)
                if g == 7 and has_r:
                    finish_base(r, odd)

        over_tiles(V, step)

        after(V, "run_counted", T - 1)
        V.scalar_tensor_tensor(out=cnt[:, :], in0=iota_e[:, :], scalar=-float(CAP), in1=run[:, :],
                               op0=ALU.mult, op1=ALU.add).then_inc(ev("table_step"), 1)
        V.wait_ge(ev("table_step"), 1)
        V.wait_ge(ev("w_cut"), T)
        V.tensor_tensor(over, cnt[:, :].unsqueeze(2).broadcast_to([P, E, T]),
                        thr[:, :].unsqueeze(1).broadcast_to([P, E, T]), ALU.is_gt).then_inc(ev("table_step"), 1)
        V.wait_ge(ev("table_step"), 2)
        V.tensor_reduce(nblk[:, :], over, AX_X, ALU.add).then_inc(ev("table_step"), 1)
        V.wait_ge(ev("table_step"), 3)
        V.wait_ge(ev("tri_made"), 1)
        V.tensor_tensor(tmp3, tri[:, :, :], nblk[:, :].unsqueeze(1).broadcast_to([P, E, E]), ALU.mult)\
         .then_inc(ev("table_step"), 1)
        V.wait_ge(ev("table_step"), 4)
        V.tensor_reduce(cum[:, :], tmp3, AX_X, ALU.add).then_inc(ev("table_step"), 1)
        V.wait_ge(ev("table_step"), 5)
        V.tensor_scalar(cum[:, :], cum[:, :], iota_p[:, 0:1], None, ALU.is_le).then_inc(ev("table_step"), 1)
        V.wait_ge(ev("table_step"), 6)
        V.tensor_reduce(tbl[:, 0:1], cum[:, :], AX_X, ALU.add).then_inc(ev("table_step"), 1)
        V.tensor_tensor_reduce(out=junk[:, 0, :], in0=cum[:, :], in1=nblk[:, :], scale=1.0, scalar=0.0,
                               op0=ALU.mult, op1=ALU.add, accum_out=tbl[:, 1:2]).then_inc(ev("table_step"), 1)
        V.wait_ge(ev("table_step"), 8)
        V.tensor_scalar(tbl[:, 2:3], iota_p[:, 0:1], tbl[:, 1:2], float(P), ALU.subtract, ALU.mult)\
         .then_inc(ev("table_step"), 1)
        V.wait_ge(ev("table_step"), 9)
        V.wait_ge(ev("table_step"), 7)
        V.scalar_tensor_tensor(out=tbl[:, 3:4], in0=tbl[:, 0:1], scalar=float(CAP), in1=tbl[:, 2:3],
                               op0=ALU.mult, op1=ALU.add).then_inc(ev("table_step"), 1)
        V.tensor_scalar(tabi[:, 1:2], tbl[:, 0:1], float(E - 1), None, ALU.min).then_inc(ev("table_step"), 1)
        V.wait_ge(ev("table_step"), 10)
        V.wait_ge(ev("table_step"), 11)
        V.tensor_copy(tabi[:, 0:1], tbl[:, 3:4]).then_inc(ev("table_made"), 1)

        V.wait_ge(ev("table_in"), 16)
        V.wait_ge(ev("b1_in"), 16)

        def copy_tokens_T(q, r):
            after(V, "tokens_T", blk(q, r))
            if not isinstance(q, int) or blk(q, r) >= 2:
                after(V, "hidden", blk(q, r) - 2)
            V.tensor_copy(xgT[:, r % 2, :], q_x[r % 2][:, 0:2 * D]).then_inc(ev("tokens_T_copied"), 1)

        def bias1(q, r):
            e = V.value_load(tab[0:1, bass.ds(blk(q, r) * 2 + 1, 1)], min_val=0, max_val=E - 1)
            after(V, "hidden", blk(q, r))
            if not isinstance(q, int) or blk(q, r) >= 2:
                after(V, "gelued", blk(q, r) - 2)
            V.scalar_tensor_tensor(out=hb[r % 2], in0=q_h[r % 2][:, :], scalar=1.0 / (SX * SW),
                                   in1=b1all[:, bass.ds(e * H, H)],
                                   op0=ALU.mult, op1=ALU.add).then_inc(ev("biased"), 1)

        def cut_low(q, r):
            after(V, "high_cut", blk(q, r))
            V.scalar_tensor_tensor(out=hl[:, r % 2, :], in0=q_g[r % 2][:, :], scalar=SH, in1=hh[:, r % 2, :],
                                   op0=ALU.mult, op1=ALU.subtract).then_inc(ev("low_cut"), 1)

        def weigh(q, r):
            after(V, "expert_out", blk(q, r))
            if not isinstance(q, int) or blk(q, r) >= 4:
                landed4(V, stored, *shift(q, r, -4))
            V.scalar_tensor_tensor(out=orow[r % 4], in0=q_o[r % 2][:, 0:D], scalar=info[:, r, 2:3].bitcast(F32),
                                   in1=xg[r % 4][:, D:2 * D], op0=ALU.mult, op1=ALU.add)\
             .then_inc(ev("weighted"), 1)

        copy_tokens_T(0, 0)

        def bstep(q, r):
            prev, nxt = shift(q, r, -1), shift(q, r, 1)
            if exists(*prev):
                cut_low(*prev)
            if exists(q, r):
                bias1(q, r)
            if exists(*nxt):
                copy_tokens_T(*nxt)
            if exists(*prev):
                weigh(*prev)

        over_blocks(V, bstep)

        for k in range(FC):
            landed(V, y_in, k // 4, k % 4)
            if k >= 4:
                landed(V, y_out, k // 4 - 1, k % 4)
            y = ybuf[k % 4].rearrange("p (j s d) -> p j s d", s=TOPK, d=D)
            V.tensor_tensor(obuf[k % 4].rearrange("p (j d) -> p j d", d=D), y[:, :, 0, :], y[:, :, 1, :], ALU.add)\
             .then_inc(ev("summed"), 1)

    @block.gpsimd
    def _(pool):
        L = pool
        L.memset(ones16[:, :], 1.0).then_inc(ev("p_ones16"), 1)
        L.memset(id32[:, :], 0.0).then_inc(ev("p_id32"), 1)
        L.wait_ge(ev("p_id32"), 1)
        L.affine_select(out=id32[:, :], in_=id32[:, :], compare_op=ALU.not_equal, fill=1.0, base=0,
                        pattern=[[-1, P]], channel_multiplier=1).then_inc(ev("p_id32"), 1)
        L.wait_ge(ev("p_id32"), 2)
        L.tensor_copy(id16[:, :], id32[:, :]).then_inc(ev("constants"), 1)
        L.wait_ge(ev("p_ones16"), 1)
        L.affine_select(out=before[:, :], in_=ones16[:, :], compare_op=ALU.is_gt, fill=0.0, base=0,
                        pattern=[[1, P]], channel_multiplier=-1).then_inc(ev("constants"), 1)
        L.iota(iota_e[:, :], [[1, E]], base=0, channel_multiplier=0, allow_small_or_imprecise_dtypes=True)\
         .then_inc(ev("constants"), 1)
        L.iota(iota_p[:, :], [[0, 1]], base=0, channel_multiplier=1, allow_small_or_imprecise_dtypes=True)\
         .then_inc(ev("constants"), 1)
        L.iota(tok[:, :, 0], [[0, TOPK]], base=0, channel_multiplier=1, allow_small_or_imprecise_dtypes=True)\
         .then_inc(ev("constants"), 1)
        L.iota(tok[:, :, 1], [[1, TOPK]], base=0, channel_multiplier=TOPK, allow_small_or_imprecise_dtypes=True)\
         .then_inc(ev("constants"), 1)
        L.memset(tok_step[:, :, 0], float(P)).then_inc(ev("constants"), 1)
        L.memset(tok_step[:, :, 1], float(P * TOPK)).then_inc(ev("constants"), 1)
        L.iota(run[:, :], [[CAP, E]], base=0, channel_multiplier=0, allow_small_or_imprecise_dtypes=True)\
         .then_inc(ev("constants"), 1)
        L.iota(thr[:, :], [[P, T]], base=0, channel_multiplier=0, allow_small_or_imprecise_dtypes=True)\
         .then_inc(ev("constants"), 1)
        L.memset(mhalf[:, :], -0.5).then_inc(ev("constants"), 1)
        L.memset(place[:, :, :], 0).then_inc(ev("constants"), 1)
        Q = E * CAP // P
        L.memset(pads[:, :, :], 0).then_inc(ev("pads_zero"), 1)
        L.memset(pads2[:, :, :], 0).then_inc(ev("pads_zero"), 1)
        L.wait_ge(ev("pads_zero"), 2)
        for w, first in ((0, N), (1, TOPK * N)):
            L.iota(pads[:, :, w], [[0, Q // P], [1, P]], base=first, channel_multiplier=0).then_inc(ev("constants"), 1)
            L.iota(pads2[:, :, w], [[0, SPARE]], base=first, channel_multiplier=1).then_inc(ev("constants"), 1)

        def rstd0(c):
            after(L, "var_ready", c)
            L.tensor_tensor(rstd[:, c * XT:(c + 1) * XT], var8[:, c, :], mhalf[:, :], ALU.pow)\
             .then_inc(ev("rstd_made"), 1)

        def low0(c):
            after(L, "xh_made", c)
            src = (xin if c < 2 else xin2)[:, (c % 2) * XT:(c % 2 + 1) * XT, :]
            L.tensor_tensor(xl[:, c * XT:(c + 1) * XT, :], src, xh[:, c * XT:(c + 1) * XT, 0:D], ALU.subtract)\
             .then_inc(ev("xparts_made"), 1)

        rstd0(0)
        for c in range(XC):
            if c + 1 < XC:
                rstd0(c + 1)
            low0(c)

        L.wait_ge(ev("constants"), CONSTANTS)
        L.dma_start(lists[0:E * CAP, :].rearrange("(p q) w -> p q w", q=Q), pads).then_inc(ev("lists_filled"), 16)
        L.dma_start(lists[E * CAP:PLACES, :].rearrange("(q p) w -> p q w", p=P), pads2)\
         .then_inc(ev("lists_filled"), 16)
        L.wait_ge(ev("zeros_made"), 1)
        L.dma_start(feats[N:N + P, :], zrow).then_inc(ev("spare_rows"), 16)
        L.wait_ge(ev("lists_filled"), 32)
        L.wait_ge(ev("ones_made"), 1)
        L.wait_ge(ev("xparts_made"), XC)

        def cut_weights(t, odd, e):
            after(L, "w_scaled", t)
            high, low = ((w1h, w1l), (w2h, w2l))[odd]
            n = DC * H
            L.tensor_tensor(low[:, bass.ds(e * n, n)], wst[:, :], high[:, bass.ds(e * n, n)], ALU.subtract)\
             .then_inc(ev("w_cut"), 1)

        def rstd1(s):
            after(L, "x1_var", s)
            L.tensor_tensor(vr[:, 1:2], vr[:, 0:1], mhalf[:, 0:1], ALU.pow).then_inc(ev("x1_rstd"), 1)

        def store_feats(s):
            after(L, "high_made", s)
            L.tensor_tensor(pay[:, D:2 * D], xf[:, :], pay[:, 0:D], ALU.subtract).then_inc(ev("low_made"), 1)
            after(L, "low_made", s)
            L.dma_start(feats[bass.ds(s * P, P), 0:D], pay[:, :].bitcast(F32)).then_inc(ev("feats_out"), 16)

        def list_tokens(s):
            after(L, "placed", s)
            after(L, "rows_put", s)
            after(L, "weight_put", s)
            passed(L)
            for k in range(TOPK):
                L.indirect_dma_start(lists, bass.IndirectOffsetOnAxis(ap=posi[:, k:k + 1].bitcast(U32), axis=0),
                                     place[:, k, :], None).then_inc(ev("listed"), 16)

        def store_base(s, odd):
            after(L, "base_made", s)
            L.dma_start(feats[bass.ds(s * P, P), D:2 * D], base[:, odd, :]).then_inc(ev("base_out"), 16)

        def step(t, odd, e):
            s, r = t - 1, t - 2
            if is_(t, lambda t: t < T):
                cut_weights(t, odd, e)
            if is_(s, lambda s: 0 <= s < T):
                rstd1(s)
            if is_(r, lambda r: 0 <= r < T):
                list_tokens(r)
            if is_(s, lambda s: 0 <= s < T):
                store_feats(s)
            if is_(r, lambda r: 0 <= r < T):
                store_base(r, odd)

        for t in (0, 1):
            step(t, t, 0)
        with L.Fori(1, T // 2 - 1) as i:
            step(i * 2, 0, i)
            step(i * 2 + 1, 1, i)
        for t in range(T - 2, T + 2):
            step(t, t % 2, t // 2)

        L.wait_ge(ev("w_cut"), T)
        L.memset(tri, 1.0).then_inc(ev("p_tri"), 1)
        L.wait_ge(ev("p_tri"), 1)
        L.affine_select(out=tri, in_=tri, compare_op=ALU.is_ge, fill=0.0, base=0,
                        pattern=[[1, E], [-1, E]], channel_multiplier=0).then_inc(ev("tri_made"), 1)

        L.wait_ge(ev("feats_out"), 16 * T)
        L.wait_ge(ev("base_out"), 16 * T)
        L.wait_ge(ev("spare_rows"), 16)

        def gather(q, r):
            landed(L, lst_in, q, r)
            if not isinstance(q, int) or blk(q, r) >= 4:
                after(L, "weighted", blk(q, r) - 4)
            passed(L)
            L.indirect_dma_start(xg[r % 4], None, feats,
                                 bass.IndirectOffsetOnAxis(ap=info[:, r, 0:1].bitcast(U32), axis=0))\
             .then_inc(xg_in[r % 4], 16)

        def store_results(q, r):
            after(L, "weighted", blk(q, r))
            passed(L)
            L.indirect_dma_start(results, bass.IndirectOffsetOnAxis(ap=info[:, r, 1:2].bitcast(U32), axis=0),
                                 orow[r % 4], None, bounds_check=TOPK * N - 1, oob_is_err=False)\
             .then_inc(stored[r % 4], 16)

        for r in range(2):
            gather(0, r)

        def bstep(q, r):
            nxt, prev = shift(q, r, 2), shift(q, r, -1)
            if exists(*nxt):
                gather(*nxt)
            if exists(*prev):
                store_results(*prev)

        over_blocks(L, bstep)

    ctx.close()


_INS = ['x', 'adj', 'L0_gnn_W', 'L0_gnn_b', 'L0_ffn_Wr', 'L0_ffn_br', 'L0_ffn_W1', 'L0_ffn_b1', 'L0_ffn_W2', 'L0_ffn_b2']
_OUTS = [((N, D), 'float32')]


def kernel(**inputs):
    import numpy as _np
    import concourse.bacc as _bacc
    from concourse import mybir as _mybir
    from concourse.bass_utils import run_bass_kernel_spmd as _run

    nc = _bacc.Bacc("TRN2", target_bir_lowering=False, num_devices=1)
    arrays, args = {}, []
    for name in _INS:
        a = _np.ascontiguousarray(inputs[name])
        arrays[f"in_{name}_dram"] = a
        args.append(nc.dram_tensor(f"in_{name}_dram", a.shape, _mybir.dt.from_np(a.dtype), kind="ExternalInput").ap())
    for i, (shape, dtype) in enumerate(_OUTS):
        dt = _mybir.dt.from_np(_np.dtype(dtype))
        args.append(nc.dram_tensor(f"out_{i}_dram", shape, dt, kind="ExternalOutput").ap())
    build(nc, *args)
    r = _run(nc, [arrays], core_ids=[0])
    got = tuple(r.results[0][f"out_{i}_dram"] for i in range(len(_OUTS)))
    return got[0]
```

```python
from contextlib import ExitStack

import concourse.bass as bass
from concourse import mybir

ALU = mybir.AluOpType
ACT = mybir.ActivationFunctionType
AX_X = mybir.AxisListType.X
F32 = mybir.dt.float32
F16 = mybir.dt.float16
I32 = mybir.dt.int32
U32 = mybir.dt.uint32

P = 128
N = 4096
D = 256
E = 16
H = 512
TOPK = 2
T = N // P
DC = D // P
HC = H // P
CH = 4
CW = N // CH
JC = CW // P
G = 2 * CH
GRAPH = 4
XC = CH
XT = T // XC
XS = (3, 3, 3, 6)
HW = D + 2
EPS = 1e-5

CAP = N
BLOCKS = N * TOPK // P + E - 1
U = 8
ROUNDS = (BLOCKS + U - 1) // U
SPARE = ROUNDS * U - N * TOPK // P
PLACES = E * CAP + SPARE * P
LW = 8

SX = 2.0 ** 11
SW = 2.0 ** 8
SH = 2.0 ** 6


def build(nc, x, adj, gnn_W, gnn_b, Wr, br, W1, b1, W2, b2, out):
    ctx = ExitStack()

    def sb(name, shape, dt):
        return ctx.enter_context(nc.sbuf_tensor(name, shape, dt))

    def sem(name):
        return ctx.enter_context(nc.semaphore(name))

    feats = nc.dram_tensor("feats", (N + P, D), F32, kind="Internal").ap()
    lists = nc.dram_tensor("lists", (PLACES, LW), I32, kind="Internal").ap()

    w1h = sb("w1h", [P, E * DC * H], F16)
    w1l = sb("w1l", [P, E * DC * H], F16)
    w2h = sb("w2h", [P, E * HC * D], F16)
    w2l = sb("w2l", [P, E * HC * D], F16)
    xin = w2h[:, :].bitcast(F32).rearrange("p (n d) -> p n d", d=D)
    xin2 = w2l[:, :].bitcast(F32).rearrange("p (n d) -> p n d", d=D)
    pads = w1l[:, (E * DC * H - 2 * P * LW):].bitcast(I32).rearrange("p (q w) -> p q w", w=LW)
    xparts = sb("xparts", [P, T * (HW + D)], F16)
    xh = xparts[:, :].rearrange("p (n w) -> p n w", w=HW + D)[:, :, 0:HW]
    xl = xparts[:, :].rearrange("p (n w) -> p n w", w=HW + D)[:, :, HW:HW + D]
    b1all = xparts[:, 0:2 * E * H].bitcast(F32)
    abuf = sb("abuf", [P, CH * CW], F32)
    xg = [abuf[:, k * D:(k + 1) * D] for k in range(U)]
    xg16 = [g.bitcast(F16) for g in xg]
    a16 = sb("a16", [P, 2, CW], F16)
    at = sb("at", [P, 2, CW], F16)
    wst = sb("wst", [P, DC * H], F32)
    hb = [a16[:, k, :].bitcast(F32) for k in range(2)]
    hg = [wst[:, k * H:(k + 1) * H] for k in range(2)]
    xgT, hh = at[:, :, 0:2 * D], at[:, :, 2 * D:2 * D + H]
    hl = sb("hl", [P, 2, H], F16)
    info = sb("info", [P, U, 2], I32)

    wg = sb("wg", [P, 2, DC, D], F16)
    gb = sb("gb", [P, D], F32)
    wr = sb("wr", [P, DC, E], F32)
    brb = sb("brb", [P, E], F32)
    b2s = sb("b2s", [E, D], F32)
    b2l = sb("b2l", [E, D], F16)
    b2hl = sb("b2hl", [2 * E, D], F16)
    sel = sb("sel", [2 * E, E], F16)
    id32 = sb("id32", [P, P], F32)
    id16 = sb("id16", [P, P], F16)
    before = sb("before", [P, P], F16)
    ones16 = sb("ones16", [P, P], F16)
    iota_e = sb("iota_e", [P, E], F32)
    iota_p = sb("iota_p", [P, 1], F32)
    first_block = sb("first_block", [P, E], F32)
    mhalf = sb("mhalf", [P, XT], F32)
    zrow = hl[:, 0, :].bitcast(F32)

    mean = sb("mean", [P, T], F32)
    rstd = sb("rstd", [P, T], F32)
    st6 = sb("st6", [P, XC, XT, 6], F32)
    var8 = sb("var8", [P, XC, XT], F32)
    dif8 = sb("dif8", [P, XT], F32)
    minus = sb("minus", [P, T], F32)
    shift0 = sb("shift0", [P, T], F32)

    xt = sb("xt", [P, 2, D], F32)
    xs = sb("xs", [P, D], F32)
    pooled = sb("pooled", [P, D], F32)
    eT = sb("eT", [P, D], F32)
    eTh, eTl = eT[:, :].bitcast(F16)[:, 0:D], eT[:, :].bitcast(F16)[:, D:2 * D]
    xf = sb("xf", [P, D], F32)
    x1 = pooled
    feat = sb("feat", [P, 2 * D], F32)
    parts, base = feat[:, 0:D].bitcast(F16), feat[:, D:2 * D]
    orow = [xt[:, 0, :], xt[:, 1, :], eT[:, :], xs[:, :]]
    deg = sb("deg", [P, 2], F32)
    bst = sb("bst", [P, 6], F32)
    mv = sb("mv", [P, 2], F32)
    vr = sb("vr", [P, 2], F32)
    bs = sb("bs", [P, 2], F32)
    lg = sb("lg", [P, E], F32)
    ex = sb("ex", [P, E], F32)
    pr = sb("pr", [P, E], F32)
    p8 = sb("p8", [P, 8], F32)
    i8 = sb("i8", [P, 8], U32)
    sc = sb("sc", [P, 8], F32)
    i2 = sb("i2", [P, 2], F32)
    oh = sb("oh", [P, 2, E], F32)
    msk = sb("msk", [P, E], F16)
    run = sb("run", [P, E], F32)
    posb = sb("posb", [P, E], F32)
    junk = sb("junk", [P, 2, E], F32)
    posf = sb("posf", [P, 2], F32)
    posi = sb("posi", [P, 2, 2], I32)
    tok = sb("tok", [P, TOPK], F32)
    place = sb("place", [P, 2, TOPK, LW], I32)

    cnt = sb("cnt", [P, E], F32)
    nblk = sb("nblk", [P, E], F32)
    cum = sb("cum", [P, E], F32)
    tbl = sb("tbl", [P, 8], F32)
    tab = pooled[0:1, :].bitcast(I32)
    tri = st6.rearrange("p c k s -> p (c k s)").bitcast(F16)[:, 0:E * E].rearrange("p (e f) -> p e f", f=E)
    tmp3 = wst[:, 0:E * E].rearrange("p (e f) -> p e f", f=E)

    banks = [ctx.enter_context(nc.psum_tensor(f"bank{i}", [P, 512], F32)) for i in range(8)]
    ps_tp = [b[:, :].bitcast(F16) for b in banks[0:2]]
    ps_acc = banks[2:4]
    ps_T, ps_Z, ps_S, ps_R = banks[4:8]
    q_x = [b[:, :].bitcast(F16) for b in banks[0:2]]
    q_h = banks[2:4]
    q_g = banks[4:6]
    q_o = banks[6:8]

    S = {}

    def ev(name):
        if name not in S:
            S[name] = sem(name)
        return S[name]

    def after(eng, name, t):
        eng.wait_ge(ev(name), t + 1)

    def passed(eng):
        eng.sem_inc(ev("passed"), 1)

    CONSTANTS = 9
    x_in = [sem(f"x_in{c}") for c in range(XC)]
    a_in = [sem(f"a_in{c}") for c in range(CH)]
    xt_in = [sem(f"xt_in{c}") for c in range(2)]
    listed = [sem(f"listed{c}") for c in range(2)]
    lst_in = [sem(f"lst_in{c}") for c in range(U)]
    xg_in = [sem(f"xg_in{c}") for c in range(U)]

    def after_added(eng, n):
        eng.wait_ge(ev("added"), (n + 1) * 16)

    def landed(eng, sems, q, r):
        eng.wait_ge(sems[r], (q + 1) * 16)

    def x_tiles(c):
        return (xin if c < 2 else xin2)[:, (c % 2) * XT:(c % 2 + 1) * XT, :]

    x_v = x.rearrange("(n p) d -> p n d", p=P)
    wg_arrival = feat[:, :].rearrange("p (c n) -> p c n", c=DC)
    consts = [(wg_arrival, gnn_W.rearrange("(c p) n -> p c n", p=P)),
              (wr[:, :, :], Wr.rearrange("(c p) n -> p c n", p=P)),
              (b2s[:, :], b2),
              (gb[:, :], gnn_b.rearrange("(a d) -> a d", a=1).broadcast_to([P, D])),
              (brb[:, :], br.rearrange("(a d) -> a d", a=1).broadcast_to([P, E]))]

    def step_up(t, c, k):
        return t + (c + k) // CH, (c + k) % CH

    def over_tiles(eng, step):
        for t in (0, 1):
            step(t, t)
        with eng.Fori(1, T // 2 - 1) as i:
            step(i * 2, 0)
            step(i * 2 + 1, 1)
        for t in range(T - 2, T + 2):
            step(t, t % 2)

    def is_(t, cond):
        return cond(t) if isinstance(t, int) else True

    def over_blocks(eng, step):
        for r in range(U):
            step(0, r)
        with eng.Fori(1, ROUNDS - 1) as q:
            for r in range(U):
                step(q, r)
        for r in range(BLOCKS + 2 - U * (ROUNDS - 1)):
            step(ROUNDS - 1, r)

    def shift(q, r, k):
        return q + (r + k) // U, (r + k) % U

    def exists(q, r):
        return not isinstance(q, int) or 0 <= U * q + r < BLOCKS

    def blk(q, r):
        return q * U + r

    block = ctx.enter_context(nc.Block())

    @block.sync
    def _(sp):
        def load_x(c):
            sp.dma_start(x_tiles(c), x_v[:, c * XT:(c + 1) * XT, :]).then_inc(x_in[c], 16)

        def load_adj0(c):
            sp.dma_start(abuf[:, c * CW:(c + 1) * CW], adj[0:P, c * CW:(c + 1) * CW]).then_inc(a_in[c], 16)

        load_x(0)
        load_adj0(0)
        load_x(1)
        load_x(2)
        load_adj0(1)
        load_x(3)
        for dst, src in consts[0:2]:
            sp.dma_start(dst, src).then_inc(ev("consts_in"), 16)
        load_adj0(2)
        load_adj0(3)
        for dst, src in consts[2:]:
            sp.dma_start(dst, src).then_inc(ev("consts_in"), 16)

        def load_adj(t, c):
            sp.wait_ge(ev("cast"), t * CH - CH + c + 1)
            sp.dma_start(abuf[:, c * CW:(c + 1) * CW],
                         adj[bass.ds(t * P, P), c * CW:(c + 1) * CW]).then_inc(a_in[c], 16)

        def store_base(s):
            after(sp, "base_made", s)
            sp.dma_start(out[bass.ds(s * P, P), :], base).then_inc(ev("base_out"), 16)

        def load_weights(t, odd, e):
            if is_(t, lambda t: t > 0):
                after(sp, "w_cut", t - 1)
            W, c = ((W1, DC), (W2, HC))[odd]
            sp.dma_start(wst[:, :].rearrange("p (c n) -> p c n", c=c),
                         W[bass.ds(e, 1), :, :].rearrange("a (c p) n -> p (a c) n", p=P)).then_inc(ev("w_in"), 16)

        def step(t, odd, e):
            if is_(t, lambda t: t > 0):
                for c in range(CH):
                    load_adj(t, c)
            if is_(t, lambda t: t >= 3):
                store_base(t - 3)
            if is_(t, lambda t: t >= 2):
                after(sp, "x1_made", t - 2)
            sp.dma_start(xt[:, odd, :], x[bass.ds(t * P, P), :]).then_inc(xt_in[odd], 16)
            load_weights(t, odd, e)

        for t in range(4):
            step(t, t % 2, t // 2)
        with sp.Fori(2, T // 2) as i:
            step(i * 2, 0, i)
            step(i * 2 + 1, 1, i)
        store_base(T - 3)

        sp.wait_ge(ev("b2_cut"), 1)
        sp.dma_start(b2hl[E:2 * E, :], b2l[:, :]).then_inc(ev("b2_in"), 16)
        b1_v = b1.rearrange("(c e) h -> c (e h)", c=CH).unsqueeze(1)
        for c in range(CH):
            n = E * H // CH
            if c == CH - 1:
                store_base(T - 2)
            sp.wait_ge(ev("multiplied"), (T - 1) * CH + c + 1)
            sp.dma_start(b1all[:, c * n:(c + 1) * n], b1_v[c].broadcast_to([P, n])).then_inc(ev("b1_in"), 16)
        store_base(T - 1)
        sp.wait_ge(ev("table_made"), 1)
        for odd in (0, 1):
            sp.wait_ge(listed[odd], 16 * TOPK * T // 2)

        def load_list(q, r):
            if not isinstance(q, int) or q > 0:
                after_added(sp, blk(q - 1, r))
            row = sp.value_load(tab[0:1, bass.ds(blk(q, r), 1)], min_val=0, max_val=PLACES - P)
            sp.dma_start(info[:, r, :], lists[bass.ds(row, P), 0:2]).then_inc(lst_in[r], 16)

        for r in range(U):
            load_list(0, r)
        with sp.Fori(1, ROUNDS - 1) as q:
            for r in range(U):
                load_list(q, r)
        for r in range(BLOCKS - U * (ROUNDS - 1)):
            load_list(ROUNDS - 1, r)

        after_added(sp, BLOCKS - 1)

    @block.tensor
    def _(pe):
        def transposes(t, c):
            pe.wait_ge(ev("cast"), t * CH + c + 1)
            for j in range(JC):
                mm = pe.transpose(ps_tp[c % 2][:, j * P:(j + 1) * P], a16[:, c % 2, j * P:(j + 1) * P], id16[:, :])
            mm.then_inc(ev("transposed"), 1)

        def pooled_T(s):
            after(pe, "pooled", s)
            for c in range(DC):
                mm = pe.transpose(ps_T[:, c * P:(c + 1) * P], pooled[:, c * P:(c + 1) * P], id32[:, :])
            mm.then_inc(ev("pooled_T"), 1)

        def graph_out(s):
            after(pe, "pooled_T_low", s)
            n = 0
            for c in range(DC):
                high, low = eTh[:, c * P:(c + 1) * P], eTl[:, c * P:(c + 1) * P]
                for a, k in ((high, 0), (high, 1), (low, 0)):
                    mm = pe.matmul(ps_Z[:, 0:D], a, wg[:, k, c, :], start=n == 0, stop=n == 3 * DC - 1)
                    n += 1
            mm.then_inc(ev("graph_out"), 1)

        def xf_T(s):
            after(pe, "xf_made", s)
            for c in range(DC):
                mm = pe.transpose(ps_T[:, D + c * P:D + (c + 1) * P], xf[:, c * P:(c + 1) * P], id32[:, :])
            mm.then_inc(ev("xf_T"), 1)

        def logits(s):
            after(pe, "xf_T_copied", s)
            if is_(s, lambda s: s >= 1):
                after(pe, "run_counted", s - 1)
            for c in range(DC):
                mm = pe.matmul(ps_S[:, 0:E], eT[:, c * P:(c + 1) * P], wr[:, c, :], start=c == 0, stop=c == DC - 1)
            mm.then_inc(ev("logits"), 1)

        def rank(s):
            after(pe, "mask_made", s)
            pe.matmul(ps_S[:, E:2 * E], before[:, :], msk[:, :], start=True, stop=True)
            pe.matmul(ps_S[:, 2 * E:3 * E], ones16[:, :], msk[:, :], start=True, stop=True)\
              .then_inc(ev("ranked"), 1)

        def step(t, odd):
            s, r = t - 1, t - 2
            has_t = is_(t, lambda t: t < T)
            has_s = is_(s, lambda s: 0 <= s < T)
            has_r = is_(r, lambda r: 0 <= r < T)
            last = isinstance(t, int) and t == T
            for g in range(G):
                c, half = divmod(g, 2)
                if has_t and not half:
                    pe.wait_ge(ev("at_made"), t * CH + c + 1)
                    t2, c2 = step_up(t, c, 2)
                    if is_(t2, lambda t2: t2 < T):
                        transposes(t2, c2)
                    if c == 0 and is_(t, lambda t: t >= 2):
                        after(pe, "acc_read", t - 2)
                    if isinstance(t, int) and t == 0:
                        after(pe, f"x_cut{c}", 0)
                if has_t:
                    for j in range(g * JC // 2, (g + 1) * JC // 2):
                        w = at[:, c % 2, (j % JC) * P:(j % JC + 1) * P]
                        both = [lambda: pe.matmul(ps_acc[odd][:, 0:D + 1], w, xh[:, j, 0:D + 1],
                                                  start=j == 0, stop=j == T - 1),
                                lambda: pe.matmul(ps_acc[odd][:, 0:D], w, xl[:, j, :], start=False, stop=False)]
                        if j == T - 1:
                            both.reverse()
                        for product in both:
                            mm = product()
                    if half:
                        mm.then_inc(ev("multiplied"), 1)
                if g == 0 and has_r:
                    logits(r)
                if g == 1 and has_s:
                    pooled_T(s)
                if g == 7 and has_s:
                    xf_T(s)
                if g == GRAPH - 1 and has_s:
                    graph_out(s)
                if g == (7 if last else 4) and has_r:
                    rank(r)

        pe.wait_ge(ev("constants"), CONSTANTS)
        transposes(0, 0)
        transposes(0, 1)
        pe.wait_ge(ev("consts_in"), 16 * len(consts))
        over_tiles(pe, step)

        def tokens_T(q, r):
            landed(pe, xg_in, q, r)
            for c in range(2 * DC):
                mm = pe.transpose(q_x[r % 2][:, c * P:(c + 1) * P], xg16[r][:, c * P:(c + 1) * P], id16[:, :])
            mm.then_inc(ev("tokens_T"), 1)

        expert = {}

        def expert_of(q, r):
            return pe.value_load(tab[0:1, bass.ds(blk(q, r) + P, 1)], min_val=0, max_val=E - 1)

        def hidden(q, r):
            e = expert[r] = expert_of(q, r)
            after(pe, "tokens_T_copied", blk(q, r))
            n = 0
            for c in range(DC):
                high = xgT[:, r % 2, c * P:(c + 1) * P]
                low = xgT[:, r % 2, D + c * P:D + (c + 1) * P]
                wh = w1h[:, bass.ds(e * (DC * H) + c * H, H)]
                wl = w1l[:, bass.ds(e * (DC * H) + c * H, H)]
                for a, w in ((high, wh), (high, wl), (low, wh)):
                    mm = pe.matmul(q_h[r % 2][:, :], a, w, start=n == 0, stop=n == 3 * DC - 1)
                    n += 1
            mm.then_inc(ev("hidden"), 1)

        def hidden_T(q, r):
            after(pe, "gelued", blk(q, r))
            for c in range(HC):
                mm = pe.transpose(q_g[r % 2][:, c * P:(c + 1) * P], hg[r % 2][:, c * P:(c + 1) * P], id32[:, :])
            mm.then_inc(ev("hidden_T"), 1)

        def expert_out(q, r):
            e = expert[r] if r < U - 2 else expert_of(q, r)
            after(pe, "low_cut", blk(q, r))
            if not isinstance(q, int) or blk(q, r) >= 2:
                after(pe, "weighted", blk(q, r) - 2)
            n = 0
            pe.matmul(q_o[r % 2][:, 0:D], sel[:, bass.ds(e, 1)].broadcast_to([2 * E, P]), b2hl[:, :], start=True, stop=False)
            for c in range(HC):
                high, low = hh[:, r % 2, c * P:(c + 1) * P], hl[:, r % 2, c * P:(c + 1) * P]
                wh = w2h[:, bass.ds(e * (HC * D) + c * D, D)]
                wl = w2l[:, bass.ds(e * (HC * D) + c * D, D)]
                for a, w in ((high, wh), (high, wl), (low, wh)):
                    mm = pe.matmul(q_o[r % 2][:, 0:D], a, w, start=False, stop=n == 3 * HC - 1)
                    n += 1
            mm.then_inc(ev("expert_out"), 1)

        pe.wait_ge(ev("table_step"), 11)
        for k in range(2):
            mm = pe.matmul(ps_R[0:1, k * P:(k + 1) * P], tbl[:, 3 + k:4 + k], id32[:, :], start=True, stop=True)
        mm.then_inc(ev("table_T"), 1)

        pe.wait_ge(ev("table_made"), 1)
        pe.wait_ge(ev("b2_in"), 16)
        pe.wait_ge(ev("sel_made"), 3)
        tokens_T(0, 0)

        def bstep(q, r):
            prev, prev2, nxt = shift(q, r, -1), shift(q, r, -2), shift(q, r, 1)
            if exists(q, r):
                hidden(q, r)
            if exists(*nxt):
                tokens_T(*nxt)
            if exists(*prev):
                hidden_T(*prev)
            if exists(*prev2):
                expert_out(*prev2)

        over_blocks(pe, bstep)

    @block.scalar
    def _(act):
        def cast(t, c):
            landed(act, a_in, t, c)
            if is_(t, lambda t: t * CH + c >= 2):
                act.wait_ge(ev("transposed"), t * CH + c - 1)
            act.activation(a16[:, c % 2, :], abuf[:, c * CW:(c + 1) * CW], ACT.Copy).then_inc(ev("cast"), 1)

        def cut_weights(t, odd, e):
            act.wait_ge(ev("w_in"), t * 16 + 16)
            n = DC * H
            act.activation((w1h, w2h)[odd][:, bass.ds(e * n, n)], wst[:, :], ACT.Copy, scale=SW)\
               .then_inc(ev("w_high"), 1)
            after(act, "w_high", t)
            act.activation(wst[:, :], wst[:, :], ACT.Copy, scale=SW).then_inc(ev("w_scaled"), 1)

        def high_pooled_T(s):
            after(act, "pooled_T", s)
            if is_(s, lambda s: s >= 1):
                after(act, "logits", s - 1)
            act.activation(eTh, ps_T[:, 0:D], ACT.Copy, scale=0.5).then_inc(ev("pooled_T_high"), 1)

        def copy_xf_T(s):
            after(act, "xf_T", s)
            act.activation(eT[:, :], ps_T[:, D:2 * D], ACT.Copy).then_inc(ev("xf_T_copied"), 1)

        def high_part(s):
            after(act, "xf_made", s)
            if is_(s, lambda s: s >= 1):
                after(act, "feats_out", s * 16 - 1)
            act.activation(parts[:, 0:D], xf[:, :], ACT.Copy).then_inc(ev("high_made"), 1)

        def exps(s):
            after(act, "max_made", s)
            act.activation(ex[:, :], lg[:, :], ACT.Exp, scale=-1.0, bias=sc[:, 0:1], accum_out=sc[:, 1:2])\
               .then_inc(ev("exps_made"), 1)

        def make_base(s):
            after(act, "base_scale", s)
            if is_(s, lambda s: s >= 1):
                after(act, "base_out", s * 16 - 1)
            act.activation(base, x1[:, :], ACT.Identity, scale=bs[:, 0:1], bias=bs[:, 1:2])\
               .then_inc(ev("base_made"), 1)

        def normalize_x(s, odd):
            act.wait_ge(xt_in[odd], s // 2 * 16 + 16 if isinstance(s, int) else (s - odd) * 8 + 16)
            if is_(s, lambda s: s >= 1):
                after(act, "pooled", s - 1)
            act.activation(xs[:, :], xt[:, odd, :], ACT.Identity, scale=rstd[:, bass.ds(s, 1)],
                           bias=shift0[:, bass.ds(s, 1)]).then_inc(ev("xs_made"), 1)

        def scale_x(c):
            src = x_tiles(c)
            after(act, "x_shift", c)
            for k in range(XS[c], XT):
                n = c * XT + k
                last = act.activation(src[:, k, :], src[:, k, :], ACT.Identity, scale=rstd[:, n:n + 1],
                                      bias=shift0[:, n:n + 1])
            last.then_inc(ev("x_scaled"), 1)
            after(act, "x_scaled", c)
            after(act, "x_scaled_v", c)
            act.activation(xh[:, c * XT:(c + 1) * XT, 0:D], src, ACT.Copy).then_inc(ev("xh_made"), 1)

        cast(0, 0)
        scale_x(0)
        cast(0, 1)
        scale_x(1)
        cast(0, 2)
        scale_x(2)
        cast(0, 3)
        cast(1, 0)
        scale_x(3)
        act.wait_ge(ev("consts_in"), 16 * len(consts))
        act.activation(wg[:, 0, :, :], wg_arrival, ACT.Copy, scale=SW).then_inc(ev("wg_high"), 1)
        act.activation(b2hl[0:E, :], b2s[:, :], ACT.Copy, scale=SW).then_inc(ev("b2_high"), 1)

        def step(t, odd, e):
            s, r = t - 1, t - 2
            has_s = is_(s, lambda s: 0 <= s < T)
            has_r = is_(r, lambda r: 0 <= r < T)
            for g in range(G):
                if g == 0 and has_r:
                    copy_xf_T(r)
                if g == 2 and has_s:
                    high_pooled_T(s)
                if g % 2 == 0:
                    t2, c2 = step_up(t, g // 2, 3)
                    if is_(t2, lambda t2: t2 < T and (t2, c2) not in ((0, 3), (1, 0))):
                        cast(t2, c2)
                if g == 1 and has_r:
                    exps(r)
                if g == 3 and is_(t, lambda t: t < T):
                    if isinstance(t, int) and t == 1:
                        for c in range(XC):
                            after(act, f"x_cut{c}", 0)
                    cut_weights(t, odd, e)
                if g == 6 and is_(t, lambda t: t < T):
                    normalize_x(t, odd)
                if g == 7 and has_s:
                    high_part(s)
                    make_base(s)

        for t in (0, 1):
            step(t, t, 0)
        with act.Fori(1, T // 2 - 1) as i:
            step(i * 2, 0, i)
            step(i * 2 + 1, 1, i)
        for t in range(T - 2, T + 2):
            step(t, t % 2, t // 2)

        def gelu(q, r):
            after(act, "biased", blk(q, r))
            if not isinstance(q, int) or blk(q, r) >= 2:
                after(act, "hidden_T", blk(q, r) - 2)
            act.activation(hg[r % 2], hb[r % 2], ACT.Gelu).then_inc(ev("gelued"), 1)

        def cut_high(q, r):
            after(act, "hidden_T", blk(q, r))
            if not isinstance(q, int) or blk(q, r) >= 2:
                after(act, "expert_out", blk(q, r) - 2)
            act.activation(hh[:, r % 2, :], q_g[r % 2][:, :], ACT.Copy, scale=SH).then_inc(ev("high_cut"), 1)

        def bstep(q, r):
            prev = shift(q, r, -1)
            if exists(q, r):
                gelu(q, r)
            if exists(*prev):
                cut_high(*prev)

        over_blocks(act, bstep)

    @block.vector
    def _(dve):
        V = dve

        def stats(c):
            src = x_tiles(c)
            V.wait_ge(x_in[c], 16)
            for k in range(XT):
                last = V.bn_stats(st6[:, c, k, :], src[:, k, :])
            last.then_inc(ev("bn"), 1)
            after(V, "bn", c)
            m_e, m_o = st6[:, c, :, 1], st6[:, c, :, 4]
            v_e, v_o = st6[:, c, :, 2], st6[:, c, :, 5]
            V.tensor_tensor(mean[:, c * XT:(c + 1) * XT], m_e, m_o, ALU.add).then_inc(ev("mean_sum"), 1)
            V.tensor_tensor(dif8[:, :], m_e, m_o, ALU.subtract).then_inc(ev("dif"), 1)
            V.tensor_tensor(var8[:, c, :], v_e, v_o, ALU.add).then_inc(ev("var_sum"), 1)
            after(V, "mean_sum", c)
            V.tensor_scalar(minus[:, c * XT:(c + 1) * XT], mean[:, c * XT:(c + 1) * XT], -0.5, None, ALU.mult)\
             .then_inc(ev("minus_made"), 1)
            after(V, "minus_made", c)
            V.tensor_scalar(mean[:, c * XT:(c + 1) * XT], mean[:, c * XT:(c + 1) * XT], 0.5, None, ALU.mult)\
             .then_inc(ev("mean_made"), 1)
            after(V, "dif", c)
            V.tensor_tensor(dif8[:, :], dif8[:, :], dif8[:, :], ALU.mult).then_inc(ev("dif2"), 1)
            after(V, "dif2", c)
            after(V, "var_sum", c)
            V.scalar_tensor_tensor(out=var8[:, c, :], in0=dif8[:, :], scalar=D / 4.0, in1=var8[:, c, :],
                                   op0=ALU.mult, op1=ALU.add).then_inc(ev("var_made"), 1)
            after(V, "var_made", c)
            V.tensor_scalar(var8[:, c, :], var8[:, c, :], 1.0 / D, EPS, ALU.mult, ALU.add)\
             .then_inc(ev("var_eps"), 1)
            after(V, "var_eps", c)
            V.tensor_scalar(var8[:, c, :], var8[:, c, :], SX ** -2, None, ALU.mult).then_inc(ev("var_ready"), 1)

        def low_x(c):
            after(V, "xh_made", c)
            src = x_tiles(c)
            V.tensor_tensor(xl[:, c * XT:(c + 1) * XT, :], src, xh[:, c * XT:(c + 1) * XT, 0:D], ALU.subtract)\
             .then_inc(ev(f"x_cut{c}"), 1)

        V.memset(zrow, 0.0).then_inc(ev("zeros_made"), 1)
        V.memset(xh[:, :, D:D + 2], 1.0).then_inc(ev("ones_made"), 1)

        def copy_chunk(t, c):
            V.wait_ge(ev("transposed"), t * CH + c + 1)
            if is_(t, lambda t: t * CH + c >= 2):
                V.wait_ge(ev("multiplied"), t * CH + c - 1)
            V.tensor_copy(at[:, c % 2, :], ps_tp[c % 2]).then_inc(ev("at_made"), 1)

        def scale_some(c):
            src = x_tiles(c)
            after(V, "rstd_made", c)
            after(V, "mean_made", c)
            for k in range(XS[c]):
                n = c * XT + k
                last = V.tensor_scalar(src[:, k, :], src[:, k, :], mean[:, n:n + 1], rstd[:, n:n + 1],
                                       ALU.subtract, ALU.mult)
            last.then_inc(ev("x_scaled_v"), 1)

        stats(0)
        copy_chunk(0, 0)
        for c in range(1, XC):
            stats(c)
            scale_some(c - 1)
        copy_chunk(0, 1)
        scale_some(XC - 1)
        low_x(1)
        copy_chunk(0, 2)
        low_x(3)
        copy_chunk(0, 3)
        after(V, "wg_high", 0)
        V.scalar_tensor_tensor(out=wg[:, 1, :, :], in0=wg_arrival, scalar=SW, in1=wg[:, 0, :, :],
                               op0=ALU.mult, op1=ALU.subtract).then_inc(ev("wg_cut"), 1)
        after(V, "b2_high", 0)
        V.scalar_tensor_tensor(out=b2l[:, :], in0=b2s[:, :], scalar=SW, in1=b2hl[0:E, :],
                               op0=ALU.mult, op1=ALU.subtract).then_inc(ev("b2_cut"), 1)

        def pool_x(s, odd):
            V.wait_ge(ev("multiplied"), s * CH + CH)
            V.tensor_scalar(deg[:, 0:1], ps_acc[odd][:, D:D + 1], 1.0, None, ALU.max).then_inc(ev("degree"), 1)
            after(V, "degree", s)
            V.reciprocal(deg[:, 1:2], deg[:, 0:1]).then_inc(ev("dinv"), 1)
            after(V, "xs_made", s)
            if is_(s, lambda s: s >= 1):
                after(V, "base_made", s - 1)
                after(V, "xf_made", s - 1)
            V.tensor_tensor(pooled[:, :], ps_acc[odd][:, 0:D], xs[:, :], ALU.add).then_inc(ev("acc_read"), 1)
            after(V, "acc_read", s)
            after(V, "dinv", s)
            V.scalar_tensor_tensor(out=pooled[:, :], in0=pooled[:, :], scalar=deg[:, 1:2], in1=xs[:, :],
                                   op0=ALU.mult, op1=ALU.add).then_inc(ev("pooled"), 1)

        def low_pooled_T(s):
            after(V, "pooled_T_high", s)
            V.scalar_tensor_tensor(out=eTl, in0=ps_T[:, 0:D], scalar=0.5, in1=eTh,
                                   op0=ALU.mult, op1=ALU.subtract).then_inc(ev("pooled_T_low"), 1)

        def graph_add(s, odd):
            after(V, "graph_out", s)
            V.scalar_tensor_tensor(out=x1[:, :], in0=ps_Z[:, 0:D], scalar=2.0 / (SX * SW), in1=gb[:, :],
                                   op0=ALU.mult, op1=ALU.add).then_inc(ev("graph_biased"), 1)
            after(V, "graph_biased", s)
            V.scalar_tensor_tensor(out=x1[:, :], in0=x1[:, :], scalar=0.0, in1=xt[:, odd, :],
                                   op0=ALU.max, op1=ALU.add).then_inc(ev("x1_made"), 1)
            after(V, "x1_made", s)
            V.bn_stats(bst[:, :], x1[:, :]).then_inc(ev("x1_stats"), 1)
            after(V, "x1_stats", s)
            passed(V)
            V.bn_aggr(mv[:, :], bst[:, :]).then_inc(ev("x1_aggr"), 1)
            after(V, "x1_aggr", s)
            V.tensor_scalar(vr[:, 0:1], mv[:, 1:2], EPS, SX ** -2, ALU.add, ALU.mult).then_inc(ev("x1_var"), 1)

        def norm_x1(s):
            after(V, "x1_rstd", s)
            if is_(s, lambda s: s >= 1):
                after(V, "xf_T", s - 1)
                after(V, "high_made", s - 1)
                after(V, "low_made", s - 1)
            V.tensor_scalar(xf[:, :], x1[:, :], mv[:, 0:1], vr[:, 1:2], ALU.subtract, ALU.mult)\
             .then_inc(ev("xf_made"), 1)
            after(V, "xf_made", s)
            if is_(s, lambda s: s >= 1):
                after(V, "base_made", s - 1)
            V.tensor_scalar(bs[:, 0:1], vr[:, 1:2], 1.0 / SX, 1.0, ALU.mult, ALU.add).then_inc(ev("base_scale0"), 1)
            after(V, "base_scale0", s)
            V.tensor_scalar(bs[:, 1:2], mv[:, 0:1], vr[:, 1:2], -1.0 / SX, ALU.mult, ALU.mult)\
             .then_inc(ev("base_scale"), 1)

        def top1(s):
            after(V, "logits", s)
            V.scalar_tensor_tensor(out=lg[:, :], in0=ps_S[:, 0:E], scalar=-1.0 / SX, in1=brb[:, :],
                                   op0=ALU.mult, op1=ALU.subtract).then_inc(ev("lg_made"), 1)
            after(V, "lg_made", s)
            V.tensor_reduce(sc[:, 0:1], lg[:, :], AX_X, ALU.min).then_inc(ev("max_made"), 1)

        def top2(s):
            after(V, "exps_made", s)
            V.reciprocal(sc[:, 2:3], sc[:, 1:2]).then_inc(ev("sum_inv"), 1)
            after(V, "sum_inv", s)
            V.tensor_scalar(pr[:, :], ex[:, :], sc[:, 2:3], None, ALU.mult).then_inc(ev("probs"), 1)
            after(V, "probs", s)
            passed(V)
            V.max(p8[:, :], pr[:, :]).then_inc(ev("top_p"), 1)
            after(V, "top_p", s)
            passed(V)
            V.max_index(i8[:, :], p8[:, :], pr[:, :]).then_inc(ev("top_i"), 1)
            V.tensor_scalar(sc[:, 3:4], p8[:, 0:1], p8[:, 1:2], 1e-9, ALU.add, ALU.max).then_inc(ev("top_sum"), 1)
            after(V, "top_sum", s)
            V.reciprocal(sc[:, 4:5], sc[:, 3:4]).then_inc(ev("top_inv"), 1)
            after(V, "top_i", s)
            V.tensor_copy(i2[:, :], i8[:, 0:2]).then_inc(ev("top_if"), 1)
            after(V, "top_inv", s)
            V.tensor_scalar(sc[:, 5:7], p8[:, 0:2], sc[:, 4:5], None, ALU.mult).then_inc(ev("top_w"), 1)
            after(V, "top_if", s)
            V.tensor_scalar(oh[:, 0, :], iota_e[:, :], i2[:, 0:1], None, ALU.is_equal).then_inc(ev("hot0"), 1)
            V.tensor_scalar(oh[:, 1, :], iota_e[:, :], i2[:, 1:2], None, ALU.is_equal).then_inc(ev("hot1"), 1)
            after(V, "hot1", s)
            after(V, "hot0", s)
            V.tensor_tensor(msk[:, :], oh[:, 0, :], oh[:, 1, :], ALU.add).then_inc(ev("mask_made"), 1)

        def count_tokens(s):
            after(V, "ranked", s)
            V.tensor_tensor(posb[:, :], ps_S[:, E:2 * E], run[:, :], ALU.add).then_inc(ev("place_base"), 1)
            after(V, "place_base", s)
            V.tensor_tensor(run[:, :], ps_S[:, 2 * E:3 * E], run[:, :], ALU.add).then_inc(ev("run_counted"), 1)

        def put_places(s, odd):
            for k in range(TOPK):
                V.tensor_tensor_reduce(out=junk[:, k, :], in0=posb[:, :], in1=oh[:, k, :], scale=1.0, scalar=0.0,
                                       op0=ALU.mult, op1=ALU.add, accum_out=posf[:, k:k + 1])\
                 .then_inc(ev(f"place{k}"), 1)
            if is_(s, lambda s: s >= 1):
                after(V, "token_next", s - 1)
            if is_(s, lambda s: s >= 2):
                V.wait_ge(listed[odd], (s - odd) // 2 * 32 if isinstance(s, int) else (s - odd) * 16)
            V.tensor_copy(place[:, odd, :, 0], tok[:, :]).then_inc(ev("rows_put"), 1)
            V.tensor_scalar(place[:, odd, :, 1].bitcast(F32), sc[:, 5:7], 1.0 / (SH * SW), None, ALU.mult)\
             .then_inc(ev("weight_put"), 1)
            after(V, "place0", s)
            after(V, "place1", s)
            V.tensor_copy(posi[:, odd, :], posf[:, :]).then_inc(ev("placed"), 1)
            after(V, "rows_put", s)
            V.tensor_scalar(tok[:, :], tok[:, :], float(P), None, ALU.add).then_inc(ev("token_next"), 1)

        V.wait_ge(ev("constants"), CONSTANTS)
        V.wait_ge(ev("consts_in"), 16 * len(consts))

        def step(t, odd):
            s, r = t - 1, t - 2
            has_s = is_(s, lambda s: 0 <= s < T)
            has_r = is_(r, lambda r: 0 <= r < T)
            last = isinstance(t, int) and t == T
            for g in range(G):
                if g % 2 == 0:
                    t2, c2 = step_up(t, g // 2, 1)
                    if is_(t2, lambda t2: t2 < T and (t2, c2) not in ((0, 1), (0, 2), (0, 3))):
                        copy_chunk(t2, c2)
                if g == 0 and has_s:
                    pool_x(s, 1 - odd)
                if g == 1 and has_r:
                    top1(r)
                if g == 2 and has_s:
                    low_pooled_T(s)
                if g == (6 if last else 2) and has_r:
                    if last:
                        norm_x1(s)
                    top2(r)
                if g == GRAPH and has_s:
                    graph_add(s, 1 - odd)
                if g == (6 if last else 5) and has_r:
                    count_tokens(r)
                if g == 6 and has_s and not last:
                    norm_x1(s)
                if g == 6 and has_r:
                    put_places(r, odd)

        over_tiles(V, step)

        after(V, "run_counted", T - 1)
        V.tensor_scalar(cnt[:, :], run[:, :], P / 2 - 0.5, 1.0 / P, ALU.add, ALU.mult).then_inc(ev("table_step"), 1)
        V.wait_ge(ev("table_step"), 1)
        V.tensor_scalar(cnt[:, :], cnt[:, :], 2.0 ** 23, None, ALU.add).then_inc(ev("table_step"), 1)
        V.wait_ge(ev("table_step"), 2)
        V.scalar_tensor_tensor(out=nblk[:, :], in0=cnt[:, :], scalar=2.0 ** 23, in1=first_block[:, :],
                               op0=ALU.subtract, op1=ALU.subtract).then_inc(ev("table_step"), 1)
        V.wait_ge(ev("table_step"), 3)
        V.wait_ge(ev("w_cut"), T)
        after(V, "tri_made", 0)
        V.tensor_tensor(tmp3, tri, nblk[:, :].unsqueeze(1).broadcast_to([P, E, E]), ALU.mult)\
         .then_inc(ev("table_step"), 1)
        V.wait_ge(ev("table_step"), 4)
        V.tensor_reduce(cum[:, :], tmp3, AX_X, ALU.add).then_inc(ev("table_step"), 1)
        V.wait_ge(ev("table_step"), 5)
        V.tensor_scalar(cum[:, :], cum[:, :], iota_p[:, 0:1], None, ALU.is_le).then_inc(ev("table_step"), 1)
        V.wait_ge(ev("table_step"), 6)
        V.tensor_reduce(tbl[:, 0:1], cum[:, :], AX_X, ALU.add).then_inc(ev("table_step"), 1)
        V.tensor_tensor_reduce(out=junk[:, 0, :], in0=cum[:, :], in1=nblk[:, :], scale=1.0, scalar=0.0,
                               op0=ALU.mult, op1=ALU.add, accum_out=tbl[:, 1:2]).then_inc(ev("table_step"), 1)
        V.wait_ge(ev("table_step"), 8)
        V.tensor_scalar(tbl[:, 4:5], tbl[:, 0:1], float(E - 1), None, ALU.min).then_inc(ev("table_step"), 1)
        V.tensor_scalar(tbl[:, 2:3], iota_p[:, 0:1], tbl[:, 1:2], float(P), ALU.subtract, ALU.mult)\
         .then_inc(ev("table_step"), 1)
        V.wait_ge(ev("table_step"), 10)
        V.scalar_tensor_tensor(out=tbl[:, 3:4], in0=tbl[:, 0:1], scalar=float(CAP), in1=tbl[:, 2:3],
                               op0=ALU.mult, op1=ALU.add).then_inc(ev("table_step"), 1)
        after(V, "table_T", 0)
        V.tensor_copy(tab[:, :], ps_R[0:1, 0:2 * P]).then_inc(ev("table_made"), 1)

        after(V, "table_made", 0)
        V.wait_ge(ev("b1_in"), 16 * CH)

        def copy_tokens_T(q, r):
            after(V, "tokens_T", blk(q, r))
            if not isinstance(q, int) or blk(q, r) >= 2:
                after(V, "hidden", blk(q, r) - 2)
            V.tensor_copy(xgT[:, r % 2, :], q_x[r % 2][:, 0:2 * D]).then_inc(ev("tokens_T_copied"), 1)

        def expert_of(q, r):
            return V.value_load(tab[0:1, bass.ds(blk(q, r) + P, 1)], min_val=0, max_val=E - 1)

        def bias1(q, r, e):
            after(V, "hidden", blk(q, r))
            if not isinstance(q, int) or blk(q, r) >= 2:
                after(V, "gelued", blk(q, r) - 2)
            V.scalar_tensor_tensor(out=hb[r % 2], in0=q_h[r % 2][:, :], scalar=1.0 / (SX * SW),
                                   in1=b1all[:, bass.ds(e * H, H)],
                                   op0=ALU.mult, op1=ALU.add).then_inc(ev("biased"), 1)

        def cut_low(q, r):
            after(V, "high_cut", blk(q, r))
            V.scalar_tensor_tensor(out=hl[:, r % 2, :], in0=q_g[r % 2][:, :], scalar=SH, in1=hh[:, r % 2, :],
                                   op0=ALU.mult, op1=ALU.subtract).then_inc(ev("low_cut"), 1)

        def weigh(q, r):
            after(V, "expert_out", blk(q, r))
            if not isinstance(q, int) or blk(q, r) >= 4:
                after_added(V, blk(q, r) - 4)
            V.tensor_scalar(orow[r % 4], q_o[r % 2][:, 0:D], info[:, r, 1:2].bitcast(F32), None, ALU.mult)\
             .then_inc(ev("weighted"), 1)

        copy_tokens_T(0, 0)

        def bstep(q, r):
            prev, prev2, nxt = shift(q, r, -1), shift(q, r, -2), shift(q, r, 1)
            if exists(q, r):
                e = expert_of(q, r)
            if exists(*nxt):
                copy_tokens_T(*nxt)
            if exists(q, r):
                bias1(q, r, e)
            if exists(*prev):
                cut_low(*prev)
            if exists(*prev2):
                weigh(*prev2)

        over_blocks(V, bstep)

    @block.gpsimd
    def _(pool):
        L = pool
        L.memset(ones16[:, :], 1.0).then_inc(ev("p_ones16"), 1)
        L.memset(id32[:, :], 0.0).then_inc(ev("p_id32"), 1)
        L.wait_ge(ev("p_id32"), 1)
        L.affine_select(out=id32[:, :], in_=id32[:, :], compare_op=ALU.not_equal, fill=1.0, base=0,
                        pattern=[[-1, P]], channel_multiplier=1).then_inc(ev("p_id32"), 1)
        L.wait_ge(ev("p_id32"), 2)
        L.tensor_copy(id16[:, :], id32[:, :]).then_inc(ev("constants"), 1)
        L.wait_ge(ev("p_ones16"), 1)
        L.affine_select(out=before[:, :], in_=ones16[:, :], compare_op=ALU.is_gt, fill=0.0, base=0,
                        pattern=[[1, P]], channel_multiplier=-1).then_inc(ev("constants"), 1)
        L.iota(iota_e[:, :], [[1, E]], base=0, channel_multiplier=0, allow_small_or_imprecise_dtypes=True)\
         .then_inc(ev("constants"), 1)
        L.iota(iota_p[:, :], [[0, 1]], base=0, channel_multiplier=1, allow_small_or_imprecise_dtypes=True)\
         .then_inc(ev("constants"), 1)
        L.iota(tok[:, :], [[0, TOPK]], base=0, channel_multiplier=1, allow_small_or_imprecise_dtypes=True)\
         .then_inc(ev("constants"), 1)
        L.iota(run[:, :], [[CAP, E]], base=0, channel_multiplier=0, allow_small_or_imprecise_dtypes=True)\
         .then_inc(ev("constants"), 1)
        L.iota(first_block[:, :], [[CAP // P, E]], base=0, channel_multiplier=0, allow_small_or_imprecise_dtypes=True)\
         .then_inc(ev("constants"), 1)
        L.memset(mhalf[:, :], -0.5).then_inc(ev("constants"), 1)
        L.memset(place[:, :, :, :], 0).then_inc(ev("constants"), 1)
        L.memset(sel[:, :], 0.0).then_inc(ev("sel_made"), 1)
        for k in range(2):
            L.wait_ge(ev("sel_made"), 1 + k)
            L.affine_select(out=sel[:, :], in_=sel[:, :], compare_op=ALU.not_equal, fill=SH, base=-E * k,
                            pattern=[[-1, E]], channel_multiplier=1).then_inc(ev("sel_made"), 1)
        L.memset(pads, 0).then_inc(ev("pads_zero"), 1)
        after(L, "pads_zero", 0)
        L.iota(pads[:, :, 0], [[1, P]], base=N, channel_multiplier=0).then_inc(ev("pads_made"), 1)

        def rstd0(c):
            after(L, "var_ready", c)
            cols = slice(c * XT, (c + 1) * XT)
            L.tensor_tensor(rstd[:, cols], var8[:, c, :], mhalf[:, :], ALU.pow).then_inc(ev("rstd_made"), 1)
            after(L, "rstd_made", c)
            after(L, "minus_made", c)
            L.tensor_tensor(shift0[:, cols], minus[:, cols], rstd[:, cols], ALU.mult).then_inc(ev("x_shift"), 1)

        def low_x(c):
            after(L, "xh_made", c)
            src = x_tiles(c)
            L.tensor_tensor(xl[:, c * XT:(c + 1) * XT, :], src, xh[:, c * XT:(c + 1) * XT, 0:D], ALU.subtract)\
             .then_inc(ev(f"x_cut{c}"), 1)

        rstd0(0)
        rstd0(1)
        low_x(0)
        rstd0(2)
        rstd0(3)
        FILL = E * CAP // P // P

        def fill_lists(first, last):
            for a in range(first, last):
                places = slice(a * P * P, (a + 1) * P * P)
                L.dma_start(lists[places, :].rearrange("(p q) w -> p q w", q=P), pads).then_inc(ev("lists_filled"), 16)

        after(L, "pads_made", 0)
        fill_lists(0, 2)
        low_x(2)

        L.wait_ge(ev("zeros_made"), 1)
        L.dma_start(feats[N:N + P, :], zrow).then_inc(ev("spare_rows"), 16)
        L.wait_ge(ev("constants"), CONSTANTS)
        L.wait_ge(ev("ones_made"), 1)
        L.memset(tri, 1.0).then_inc(ev("tri_ones"), 1)
        after(L, "tri_ones", 0)
        L.affine_select(out=tri, in_=tri, compare_op=ALU.is_ge, fill=0.0, base=0,
                        pattern=[[1, E], [-1, E]], channel_multiplier=0).then_inc(ev("tri_made"), 1)
        for c in range(XC):
            after(L, f"x_cut{c}", 0)

        def cut_weights(t, odd, e):
            after(L, "w_scaled", t)
            high, low = ((w1h, w1l), (w2h, w2l))[odd]
            n = DC * H
            L.tensor_tensor(low[:, bass.ds(e * n, n)], wst[:, :], high[:, bass.ds(e * n, n)], ALU.subtract)\
             .then_inc(ev("w_cut"), 1)

        def rstd1(s):
            after(L, "x1_var", s)
            L.tensor_tensor(vr[:, 1:2], vr[:, 0:1], mhalf[:, 0:1], ALU.pow).then_inc(ev("x1_rstd"), 1)

        def store_feats(s):
            after(L, "high_made", s)
            L.tensor_tensor(parts[:, D:2 * D], xf[:, :], parts[:, 0:D], ALU.subtract).then_inc(ev("low_made"), 1)
            after(L, "low_made", s)
            L.dma_start(feats[bass.ds(s * P, P), :], parts.bitcast(F32)).then_inc(ev("feats_out"), 16)

        def list_tokens(s, odd):
            after(L, "placed", s)
            after(L, "rows_put", s)
            after(L, "weight_put", s)
            passed(L)
            for k in range(TOPK):
                L.indirect_dma_start(lists, bass.IndirectOffsetOnAxis(ap=posi[:, odd, k:k + 1].bitcast(U32), axis=0),
                                     place[:, odd, k, :], None).then_inc(listed[odd], 16)

        def step(t, odd, e):
            s, r = t - 1, t - 2
            if is_(t, lambda t: t < T):
                cut_weights(t, odd, e)
            if is_(s, lambda s: 0 <= s < T):
                rstd1(s)
            if is_(r, lambda r: 0 <= r < T):
                list_tokens(r, odd)
            if is_(s, lambda s: 0 <= s < T):
                store_feats(s)

        step(0, 0, 0)
        fill_lists(2, FILL)
        L.dma_start(lists[E * CAP:PLACES, :].rearrange("(p q) w -> p q w", q=P), pads[0:SPARE, :, :])\
         .then_inc(ev("lists_filled"), 16)
        step(1, 1, 0)
        L.wait_ge(ev("lists_filled"), 16 * (FILL + 1))
        with L.Fori(1, T // 2 - 1) as i:
            step(i * 2, 0, i)
            step(i * 2 + 1, 1, i)
        for t in range(T - 2, T + 2):
            step(t, t % 2, t // 2)

        L.wait_ge(ev("feats_out"), 16 * T)
        L.wait_ge(ev("spare_rows"), 16)
        L.wait_ge(ev("base_out"), 16 * T)

        def gather(q, r):
            landed(L, lst_in, q, r)
            if not isinstance(q, int) or q > 0:
                after(L, "weighted", blk(q - 1, r))
            passed(L)
            L.indirect_dma_start(xg[r], None, feats,
                                 bass.IndirectOffsetOnAxis(ap=info[:, r, 0:1].bitcast(U32), axis=0))\
             .then_inc(xg_in[r], 16)

        def add_results(q, r):
            after(L, "weighted", blk(q, r))
            if not isinstance(q, int) or blk(q, r) >= 1:
                after_added(L, blk(q, r) - 1)
            passed(L)
            L.indirect_dma_start(out, bass.IndirectOffsetOnAxis(ap=info[:, r, 0:1].bitcast(U32), axis=0),
                                 orow[r % 4], None, bounds_check=N - 1, oob_is_err=False, compute_op=ALU.add)\
             .then_inc(ev("added"), 16)

        for r in range(3):
            gather(0, r)

        def bstep(q, r):
            nxt, prev2 = shift(q, r, 3), shift(q, r, -2)
            if exists(*nxt):
                gather(*nxt)
            if exists(*prev2):
                add_results(*prev2)

        over_blocks(L, bstep)

    ctx.close()


_INS = ['x', 'adj', 'L0_gnn_W', 'L0_gnn_b', 'L0_ffn_Wr', 'L0_ffn_br', 'L0_ffn_W1', 'L0_ffn_b1', 'L0_ffn_W2', 'L0_ffn_b2']
_OUTS = [((N, D), 'float32')]


def kernel(**inputs):
    import numpy as _np
    import concourse.bacc as _bacc
    from concourse import mybir as _mybir
    from concourse.bass_utils import run_bass_kernel_spmd as _run

    nc = _bacc.Bacc("TRN2", target_bir_lowering=False, num_devices=1)
    arrays, args = {}, []
    for name in _INS:
        a = _np.ascontiguousarray(inputs[name])
        arrays[f"in_{name}_dram"] = a
        args.append(nc.dram_tensor(f"in_{name}_dram", a.shape, _mybir.dt.from_np(a.dtype), kind="ExternalInput").ap())
    for i, (shape, dtype) in enumerate(_OUTS):
        dt = _mybir.dt.from_np(_np.dtype(dtype))
        args.append(nc.dram_tensor(f"out_{i}_dram", shape, dt, kind="ExternalOutput").ap())
    build(nc, *args)
    r = _run(nc, [arrays], core_ids=[0])
    got = tuple(r.results[0][f"out_{i}_dram"] for i in range(len(_OUTS)))
    return got[0]
```
